# Optimizing a Trainium2 kernel written in Bass

```python
import numpy as np
import jax
import jax.numpy as jnp

def _softmax(x, axis=-1):
    return jax.nn.softmax(x, axis=axis)

def _gelu(x):
    return jax.nn.gelu(x, approximate=True)

def _silu(x):
    return jax.nn.silu(x)

def _sigmoid(x):
    return jax.nn.sigmoid(x)

def _layernorm(x, axis=-1, eps=1e-05):
    m = jnp.mean(x, axis=axis, keepdims=True)
    v = jnp.var(x, axis=axis, keepdims=True)
    return (x - m) / jnp.sqrt(v + eps)

def _scatter_add(tgt, idx, src, axis=0):
    return tgt.at[idx].add(src)

def _segment_sum(src, seg, n):
    return jax.ops.segment_sum(src, seg, n)
kernel_name = 'mk_sandwich_d1_jaxref_r4_bcf184'

def setup_inputs(seed: int=0):
    np.random.seed(seed)
    _w = jnp.asarray

    def _L0_attn_setup():
        import jax, jax.numpy as jnp
        import numpy as np
        EPS = 1e-06
        CHUNK = 128

        def elu_plus_one(x):
            return jax.nn.elu(x) + 1.0

        def causal_linear_attention(q, k, v):
            B, S, D = q.shape
            sq = elu_plus_one(q)
            sk = elu_plus_one(k)
            N = S // CHUNK
            sq_c = sq.reshape(B, N, CHUNK, D).transpose(1, 0, 2, 3)
            sk_c = sk.reshape(B, N, CHUNK, D).transpose(1, 0, 2, 3)
            v_c = v.reshape(B, N, CHUNK, D).transpose(1, 0, 2, 3)
            mask = jnp.tril(jnp.ones((CHUNK, CHUNK), dtype=q.dtype))

            def step(carry, inp):
                S_kv, z = carry
                sqi, ski, vi = inp
                A = jnp.einsum('bid,bjd->bij', sqi, ski) * mask
                num = jnp.einsum('bij,bje->bie', A, vi) + jnp.einsum('bid,bde->bie', sqi, S_kv)
                den = A.sum(-1) + jnp.einsum('bid,bd->bi', sqi, z)
                out = num / jnp.clip(den, EPS, None)[..., None]
                S_kv = S_kv + jnp.einsum('bcd,bce->bde', ski, vi)
                z = z + ski.sum(axis=1)
                return ((S_kv, z), out)
            init = (jnp.zeros((B, D, D), q.dtype), jnp.zeros((B, D), q.dtype))
            _, outs = jax.lax.scan(step, init, (sq_c, sk_c, v_c))
            return outs.transpose(1, 0, 2, 3).reshape(B, S, D)
        key = jax.random.key(seed)
        ks = jax.random.split(key, 8)
        B, S, D = (2, 512, 256)
        scale = 1.0 / np.sqrt(D)
        return {'hidden_states': jax.random.normal(ks[0], (B, S, D), jnp.float32), 'w_q': jax.random.normal(ks[1], (D, D), jnp.float32) * scale, 'w_k': jax.random.normal(ks[2], (D, D), jnp.float32) * scale, 'w_v': jax.random.normal(ks[3], (D, D), jnp.float32) * scale, 'w_o': jax.random.normal(ks[4], (D, D), jnp.float32) * scale, 'gate': jnp.zeros((1,), jnp.float32), 'memory': jax.random.uniform(ks[5], (D, D), jnp.float32) * 0.01, 'memory_norm': jax.random.uniform(ks[6], (D,), jnp.float32)}
    _L0_attn_in = _L0_attn_setup()

    def _L0_ffn_setup():
        import jax, jax.numpy as jnp
        import numpy as np
        B, T, H = (2, 512, 256)
        I = 1024
        HEADS = 4
        RET = 128
        NUM_EXPERTS = 1024
        NUM_KEYS = 64
        K = 8
        key = jax.random.key(seed)
        ks = jax.random.split(key, 7)
        return {'hidden_states': jax.random.normal(ks[0], (B, T, H), jnp.float32), 'W_up': jax.random.normal(ks[1], (I, H), jnp.float32) * 0.02, 'W_down': jax.random.normal(ks[2], (H, I), jnp.float32) * 0.02, 'W_q': jax.random.normal(ks[3], (HEADS * RET, H), jnp.float32) * 0.02, 'keys': jax.random.normal(ks[4], (HEADS, NUM_KEYS, 2, RET // 2), jnp.float32) * 0.02, 'down_embed': jax.random.normal(ks[5], (NUM_EXPERTS, H), jnp.float32) * 0.02, 'up_embed': jax.random.normal(ks[6], (NUM_EXPERTS, H), jnp.float32) * 0.02}
    _L0_ffn_in = _L0_ffn_setup()
    _d = {'L0_attn_hidden_states': _L0_attn_in['hidden_states'], 'L0_attn_w_q': _L0_attn_in['w_q'], 'L0_attn_w_k': _L0_attn_in['w_k'], 'L0_attn_w_v': _L0_attn_in['w_v'], 'L0_attn_w_o': _L0_attn_in['w_o'], 'L0_attn_gate': _L0_attn_in['gate'], 'L0_attn_memory': _L0_attn_in['memory'], 'L0_attn_memory_norm': _L0_attn_in['memory_norm'], 'L0_ffn_W_up': _L0_ffn_in['W_up'], 'L0_ffn_W_down': _L0_ffn_in['W_down'], 'L0_ffn_W_q': _L0_ffn_in['W_q'], 'L0_ffn_keys': _L0_ffn_in['keys'], 'L0_ffn_down_embed': _L0_ffn_in['down_embed'], 'L0_ffn_up_embed': _L0_ffn_in['up_embed']}
    _x0 = _d['L0_attn_hidden_states']
    _d['L0_attn_hidden_states'] = jax.random.normal(jax.random.fold_in(jax.random.key(seed), 1), (8, 2048, 256), dtype=_x0.dtype)
    del _x0
    return _d

def reference(L0_attn_hidden_states, L0_attn_w_q, L0_attn_w_k, L0_attn_w_v, L0_attn_w_o, L0_attn_gate, L0_attn_memory, L0_attn_memory_norm, L0_ffn_W_up, L0_ffn_W_down, L0_ffn_W_q, L0_ffn_keys, L0_ffn_down_embed, L0_ffn_up_embed):

    def _L0_attn_ref(hidden_states, w_q, w_k, w_v, w_o, gate, memory, memory_norm):
        import jax, jax.numpy as jnp
        import numpy as np
        EPS = 1e-06
        CHUNK = 128

        def elu_plus_one(x):
            return jax.nn.elu(x) + 1.0

        def causal_linear_attention(q, k, v):
            B, S, D = q.shape
            sq = elu_plus_one(q)
            sk = elu_plus_one(k)
            N = S // CHUNK
            sq_c = sq.reshape(B, N, CHUNK, D).transpose(1, 0, 2, 3)
            sk_c = sk.reshape(B, N, CHUNK, D).transpose(1, 0, 2, 3)
            v_c = v.reshape(B, N, CHUNK, D).transpose(1, 0, 2, 3)
            mask = jnp.tril(jnp.ones((CHUNK, CHUNK), dtype=q.dtype))

            def step(carry, inp):
                S_kv, z = carry
                sqi, ski, vi = inp
                A = jnp.einsum('bid,bjd->bij', sqi, ski) * mask
                num = jnp.einsum('bij,bje->bie', A, vi) + jnp.einsum('bid,bde->bie', sqi, S_kv)
                den = A.sum(-1) + jnp.einsum('bid,bd->bi', sqi, z)
                out = num / jnp.clip(den, EPS, None)[..., None]
                S_kv = S_kv + jnp.einsum('bcd,bce->bde', ski, vi)
                z = z + ski.sum(axis=1)
                return ((S_kv, z), out)
            init = (jnp.zeros((B, D, D), q.dtype), jnp.zeros((B, D), q.dtype))
            _, outs = jax.lax.scan(step, init, (sq_c, sk_c, v_c))
            return outs.transpose(1, 0, 2, 3).reshape(B, S, D)
        q = hidden_states @ w_q.T
        k = hidden_states @ w_k.T
        v = hidden_states @ w_v.T
        sigma_q = elu_plus_one(q)
        a_mem = sigma_q @ memory
        norm = jnp.clip(sigma_q @ memory_norm, EPS, None)[..., None]
        active = (memory_norm.sum() >= EPS).astype(q.dtype)
        memory_output = active * (a_mem / norm)
        local_output = causal_linear_attention(q, k, v)
        g = jax.nn.sigmoid(gate)
        output = g * memory_output + (1.0 - g) * local_output
        return output @ w_o.T

    def _L0_ffn_ref(hidden_states, W_up, W_down, W_q, keys, down_embed, up_embed):
        import jax, jax.numpy as jnp
        import numpy as np
        B, T, H = (2, 512, 256)
        I = 1024
        HEADS = 4
        RET = 128
        NUM_EXPERTS = 1024
        NUM_KEYS = 64
        K = 8
        b, t, hd = hidden_states.shape
        h, nk, _, n = keys.shape
        q = jnp.einsum('btd,ed->bte', hidden_states, W_q)
        q = q.reshape(b, t, 2, h, n).transpose(2, 0, 1, 3, 4)
        sim = jnp.einsum('pbthn,hkpn->pbthk', q, keys)
        scores_xy, idx_xy = jax.lax.top_k(sim, K)
        sx, sy = (scores_xy[0], scores_xy[1])
        ix, iy = (idx_xy[0], idx_xy[1])
        all_scores = (sx[..., :, None] + sy[..., None, :]).reshape(b, t, h, K * K)
        all_idx = (ix[..., :, None] * nk + iy[..., None, :]).reshape(b, t, h, K * K)
        scores, pk = jax.lax.top_k(all_scores, K)
        indices = jnp.take_along_axis(all_idx, pk, axis=-1)
        de = down_embed[indices]
        ue = up_embed[indices]
        w = jax.nn.silu(jnp.einsum('btd,bthkd->bthk', hidden_states, de) * jax.nn.softmax(scores, axis=-1))
        experts_states = jnp.einsum('bthk,bthkd->btd', w, ue)
        dense = jnp.einsum('bti,di->btd', jax.nn.silu(jnp.einsum('btd,id->bti', hidden_states, W_up)), W_down)
        return dense + experts_states
    x = L0_attn_hidden_states
    x = x + _layernorm(_L0_attn_ref(_layernorm(x, axis=-1), L0_attn_w_q, L0_attn_w_k, L0_attn_w_v, L0_attn_w_o, L0_attn_gate, L0_attn_memory, L0_attn_memory_norm), axis=-1)
    x = x + _layernorm(_L0_ffn_ref(_layernorm(x, axis=-1), L0_ffn_W_up, L0_ffn_W_down, L0_ffn_W_q, L0_ffn_keys, L0_ffn_down_embed, L0_ffn_up_embed), axis=-1)
    return x

_drawn_inputs = setup_inputs


def setup_inputs(seed=0):
    import zlib

    import numpy as np

    out = dict(_drawn_inputs(seed))
    spreads = {}
    factors = {'L0_attn_memory': 200.0,
     'L0_attn_memory_norm': 200.0,
     'L0_ffn_W_q': 62.196,
     'L0_ffn_keys': 60.825}
    for name, (base, spread) in spreads.items():
        noise = np.random.default_rng([zlib.crc32(name.encode()), seed]).standard_normal(out[name].shape)
        drawn = base * np.exp(spread * noise) if base else spread * noise
        out[name] = jnp.asarray(drawn.astype(out[name].dtype))
    for name, factor in factors.items():
        out[name] = (out[name] * factor).astype(out[name].dtype)
    return out
```

```python
import concourse.bass as bass
from concourse import mybir
from contextlib import ExitStack


def sandwich_kernel(nc, hidden, w_q, w_k, w_v, w_o, gate, memory, memory_norm,
                    W_up, W_down, W_rq, keys, down_embed, up_embed, out):
    fp32 = mybir.dt.float32
    ALU = mybir.AluOpType
    ACT = mybir.ActivationFunctionType
    AX = mybir.AxisListType

    BATCH, SEQ, D = hidden.shape
    P = 128
    DC = D // P
    TILES = BATCH * SEQ // P
    CHUNKS = SEQ // P
    INNER = W_up.shape[0]
    IC = INNER // P
    HEADS, NKEYS, SIDES, KDIM = keys.shape
    GROUPS = SIDES * HEADS
    EXPERTS = down_embed.shape[0]
    EC = EXPERTS // P
    XIN = EXPERTS // NKEYS
    TOP = 8
    HALF = 512
    LAST_IN = EXPERTS - 1
    LN_EPS = 1e-5
    EPS = 1e-6
    SLOTS = 4

    x_tiles = hidden.rearrange("b (c p) d -> p c b d", p=P)
    out_tiles = out.rearrange("b (c p) d -> p c b d", p=P)

    ctx = ExitStack()
    with ctx:
        def sb(name, shape, dt=fp32):
            return ctx.enter_context(nc.sbuf_tensor(name, shape, dt))

        def sem(name):
            return ctx.enter_context(nc.semaphore(name))

        keys_in = sb("keys_in", [NKEYS, HEADS, SIDES, KDIM])
        row_in = sb("row_in", [1, 1 + D])
        wqT, wkT, woT, memT = (sb(n, [P, DC, D]) for n in ("wqT", "wkT", "woT", "memT"))
        wvo = sb("wvo", [P, DC, D])
        mem_x = sb("mem_x", [P, DC, D + 1])
        wupT = sb("wupT", [P, DC, INNER])
        deT = sb("deT", [P, DC, EXPERTS])
        wdownT = sb("wdownT", [P, IC, D])
        ue = sb("ue", [P, EC, D])
        keysT = sb("keysT", [KDIM, GROUPS, NKEYS])
        route = sb("route", [P, DC, GROUPS * NKEYS])
        ident = sb("ident", [P, P])
        causal = sb("causal", [P, P])
        ones_row = sb("ones_row", [1, P])
        minus_half = sb("minus_half", [P, 1])
        ln_eps = sb("ln_eps", [P, 1])
        gates = sb("gates", [P, 2])
        gtmp = sb("gtmp", [P, 4])

        x_in = sb("x_in", [P, SLOTS, D])
        x_mid = sb("x_mid", [P, SLOTS, D])
        x_out = sb("x_out", [P, D])
        stats = sb("stats", [P, 4, 6])
        mv = sb("mv", [P, 4, 2])
        var_eps = sb("var_eps", [P, 4])
        rstd = sb("rstd", [P, 4])
        xn1, xn2, ln_o, ln_y, mix = (sb(n, [P, D]) for n in ("xn1", "xn2", "ln_o", "ln_y", "mix"))
        xn1T, xn2T = (sb(n, [P, DC, P]) for n in ("xn1T", "xn2T"))
        eqk = sb("eqk", [P, 2 * DC, P])
        sig = sb("sig", [P, 2 * DC, P])
        z_add = sb("z_add", [P, DC])
        v_one = sb("v_one", [P, D + 1])
        sk_nat = sb("sk_nat", [P, D])
        at = sb("at", [P, P])
        dens = sb("dens", [P, 2])
        rden = sb("rden", [P, 2])
        coef = sb("coef", [P, 2])
        state = sb("state", [P, BATCH, DC, D + 1])
        scores = sb("scores", [P, GROUPS, NKEYS])
        top = sb("top", [P, GROUPS, TOP])
        x_key = sb("x_key", [P, HEADS, TOP], mybir.dt.uint32)
        clamped = sb("clamped", [P, HEADS, TOP])
        cand = sb("cand", [P, HEADS, TOP, TOP])
        best = sb("best", [P, HEADS, TOP])
        neg_max = sb("neg_max", [P, HEADS])
        NC = HEADS * TOP * TOP
        cdif = sb("cdif", [P, NC + HEADS * TOP])
        cmask = sb("cmask", [P, HEADS, TOP, TOP])
        zsum = sb("zsum", [P, HEADS])
        rz = sb("rz", [P, HEADS])
        z_last = sb("z_last", [P, NC])
        w_last = sb("w_last", [P, 1])
        down = sb("down", [P, EXPERTS])
        sums = sb("sums", [P, HEADS, XIN, NKEYS])
        prob = sb("prob", [P, HEADS, EXPERTS])
        wexp = sb("wexp", [P, HEADS, EXPERTS])
        wsum = sb("wsum", [P, EXPERTS])
        hT = sb("hT", [P, IC, P])
        gT = sb("gT", [P, EC, P])

        wq_in, wk_in, wv_in, wo_in, mem_in = (
            sums[:, :, :, :].rearrange("p h x y -> p (h x y)")[:, n * DC * D:(n + 1) * DC * D].rearrange("p (c n) -> p c n", n=D)
            for n in range(5))
        wup_in = wexp[:, 0:2, :].rearrange("p h n -> p (h n)").rearrange("p (c n) -> p c n", n=D)
        wdown_in = wexp[:, 2:4, :].rearrange("p h n -> p (h n)").rearrange("p (c n) -> p c n", n=INNER)
        de_in = prob[:, 0:2, :].rearrange("p h n -> p (h n)").rearrange("p (c n) -> p c n", n=D)
        wrq_in = prob[0:KDIM, 2:4, :].rearrange("p h n -> p (h n)").rearrange("p (c n) -> p c n", n=D)

        bank = [ctx.enter_context(nc.psum_tensor(f"bank{n}", [P, HALF], fp32)) for n in range(8)]
        t_ps = bank[0][:, 0:D]
        sk_ps = bank[0][:, D:2 * D]
        qk_ps = bank[1]
        v_ps = bank[2][:, 0:D]
        y_ps = bank[2][:, D:2 * D]
        mem_ps = bank[3][:, 0:D + 1]
        at_ps = bank[3][:, HALF - P:HALF]
        num_ps = bank[4][:, 0:D + 1]
        ds_ps = bank[5]
        even_ps, odd_ps = bank[6], bank[7]

        s_w = sem("weights_in")
        s_const = sem("constants_ready")
        s_set_ps = sem("setup_in_psum")
        s_set_sb = sem("setup_evicted")
        s_gate = sem("gate_steps")
        s_passed = sem("waits_passed")
        s_mem_x = sem("memory_norm_in")
        s_x = sem("x_loaded")
        s_stored = sem("x_stored")
        (s_xn1, s_xn1T_ps, s_xn1T, s_qk_ps, s_eqk, s_emin, s_sig, s_v_ps, s_v, s_sk_ps, s_sk, s_at_ps, s_at,
         s_mem_ps, s_num_ps, s_ds_ps, s_state, s_dens, s_rden, s_coef, s_mix_mem, s_mix, s_ln_o, s_xmid) = (
            sem(n) for n in (
                "xn1_ready", "xn1T_in_psum", "xn1T_ready", "qk_in_psum", "exp_qk_ready", "exp_capped", "sigma_ready",
                "v_in_psum", "v_ready", "sk_in_psum", "sk_ready", "scores_in_psum", "scores_masked", "mem_in_psum",
                "num_in_psum", "state_add_in_psum", "state_ready", "denominators", "denominators_inverted",
                "coefficients", "mix_memory_part", "mix_ready", "mix_normed", "x_mid_ready"))
        (s_xn2, s_xn2T_ps, s_xn2T, s_sc_ps, s_sc, s_top, s_xkey, s_clamped, s_cand, s_best, s_negm, s_cdif, s_cexp,
         s_cm1, s_cm2, s_zsum, s_rz, s_pe, s_zlast, s_d_ps, s_d, s_sum, s_prob, s_sel, s_zexp, s_u_ps) = (
            sem(n) for n in (
                "xn2_ready", "xn2T_in_psum", "xn2T_ready", "route_scores_in_psum", "route_scores_ready", "top_keys",
                "x_key_ready", "clamped_ready", "candidates_ready", "best_ready", "neg_max_ready", "differences_ready",
                "cand_exp_ready", "cand_mask_best", "cand_mask_clamped", "softmax_sums", "softmax_inverses",
                "cand_prob_ready", "last_expert_in_ready", "down_halves_in_psum", "down_halves_ready",
                "head_sums_ready", "head_probs_ready", "head_selected", "head_inputs_ready", "up_halves_in_psum"))
        (s_hT, s_wexp, s_wlast, s_w2, s_w1, s_wsum, s_g_ps, s_gT, s_y_ps, s_ln_y, s_out) = (
            sem(n) for n in (
                "hidden_halves_ready", "head_weights_ready", "last_expert_weight", "head_pairs_added", "heads_added",
                "expert_weights_ready", "expert_weights_T_in_psum", "expert_weights_T_ready", "y_in_psum",
                "y_normed", "x_out_ready"))
        LN_X, LN_O, LN_M, LN_Y = range(4)
        s_stats = [sem(f"ln_stats_{n}") for n in ("x", "o", "mid", "y")]
        s_mv = [sem(f"ln_moments_{n}") for n in ("x", "o", "mid", "y")]
        s_veps = [sem(f"ln_var_eps_{n}") for n in ("x", "o", "mid", "y")]
        s_rstd = [sem(f"ln_rstd_{n}") for n in ("x", "o", "mid", "y")]

        def wait(eng, s, value):
            if not isinstance(value, int) or value > 0:
                eng.wait_ge(s, value)

        def alone(eng):
            eng.sem_inc(s_passed, 1)

        def pipeline(eng, body):
            body(0, None, None)
            body(1, 0, None)
            body(2, 1, 0)
            with eng.Fori(3, TILES) as i:
                body(i, i - 1, i - 2)
            body(None, TILES - 1, TILES - 2)
            body(None, None, TILES - 1)

        def slot(t):
            return t % SLOTS if isinstance(t, int) else t & (SLOTS - 1)

        def seq_of(t):
            return t % BATCH if isinstance(t, int) else t & (BATCH - 1)

        def chunk_of(t):
            return t // BATCH if isinstance(t, int) else (t >> (BATCH.bit_length() - 1)) & (CHUNKS - 1)

        def square_blocks(w):
            return [w[:, rc, dc * P:(dc + 1) * P] for dc in range(DC) for rc in range(DC)]

        def tall_blocks(w, dc, half):
            return [w[:, rc, dc * P:(dc + 1) * P] for rc in range(4 * half, 4 * half + 4)]

        turned = [(square_blocks(w_in), wT[:, :, :].rearrange("p c n -> p (c n)"))
                  for w_in, wT in ((wo_in, woT), (mem_in, memT), (wq_in, wqT), (wk_in, wkT))]
        for w_in, wT in ((wup_in, wupT), (de_in, deT)):
            turned += [(tall_blocks(w_in, dc, half), wT[:, dc, half * HALF:(half + 1) * HALF])
                       for dc in range(DC) for half in range(2)]
        for pair in range(IC // 2):
            turned.append(([wdown_in[:, dc, ic * P:(ic + 1) * P] for ic in (2 * pair, 2 * pair + 1) for dc in range(DC)],
                           wdownT[:, 2 * pair:2 * pair + 2, :].rearrange("p c n -> p (c n)")))
        TURNED = len(turned)
        SET_KEYS, SET_WVO, SET_MEM, SET_ROUTE, SET_GATE = TURNED, TURNED + 1, TURNED + 2, TURNED + 3, TURNED + 3 + DC
        SET_ALL = SET_GATE + 1
        LOADS = 12

        block = ctx.enter_context(nc.Block())

        @block.sync
        def _(sp):
            for dst, src in ((wo_in, w_o), (mem_in, memory), (wq_in, w_q), (wk_in, w_k), (wv_in, w_v),
                             (wup_in, W_up), (de_in, down_embed), (wdown_in, W_down), (ue, up_embed)):
                sp.dma_start(dst[:, :, :], src.rearrange("(c p) n -> p c n", p=P)).then_inc(s_w, 16)
            sp.dma_start(wrq_in[:, :, :], W_rq.rearrange("(g n) d -> n g d", n=KDIM)).then_inc(s_w, 16)
            sp.dma_start(keys_in[:, :, :, :], keys.rearrange("h k s n -> k h s n")).then_inc(s_w, 16)
            sp.dma_start(row_in[:, 0:1], gate.rearrange("(a n) -> a n", a=1)).then_inc(s_w, 16)
            sp.dma_start(row_in[:, 1:1 + D], memory_norm.rearrange("(a n) -> a n", a=1)).then_inc(s_mem_x, 16)
            for dc in range(DC):
                sp.dma_start(mem_x[:, dc, D:D + 1],
                             memory_norm[dc * P:(dc + 1) * P].rearrange("(p a) -> p a", a=1)).then_inc(s_mem_x, 16)

            def load(t):
                wait(sp, s_xmid, t - SLOTS + 1)
                wait(sp, s_x, 16 * t)
                alone(sp)
                sp.dma_start(x_in[:, slot(t), :], x_tiles[:, chunk_of(t), seq_of(t), :]).then_inc(s_x, 16)

            def store(t):
                sp.wait_ge(s_out, t + 1)
                alone(sp)
                sp.dma_start(out_tiles[:, chunk_of(t), seq_of(t), :], x_out[:, :]).then_inc(s_stored, 16)

            AHEAD = 2
            for t in range(2 + AHEAD):
                load(t)
            with sp.Fori(2, TILES - AHEAD) as i:
                load(i + AHEAD)
                store(i - 2)
            for t in range(TILES - AHEAD - 2, TILES):
                store(t)
            sp.wait_ge(s_stored, 16 * TILES)

        @block.gpsimd
        def _(pool):
            nc.gpsimd.memset(ident[:, :], 0.0).then_inc(s_const, 1)
            nc.gpsimd.memset(causal[:, :], 1.0).then_inc(s_const, 1)
            nc.gpsimd.memset(minus_half[:, :], -0.5).then_inc(s_const, 1)
            nc.gpsimd.memset(ln_eps[:, :], LN_EPS).then_inc(s_const, 1)
            nc.gpsimd.memset(ones_row[:, :], 1.0).then_inc(s_const, 1)
            nc.gpsimd.memset(v_one[:, D:D + 1], 1.0).then_inc(s_const, 1)
            for b in range(BATCH):
                nc.gpsimd.memset(state[:, b, :, :], 0.0).then_inc(s_state, 1)
            pool.wait_ge(s_const, 6)
            nc.gpsimd.affine_select(out=ident[:, :], in_=ident[:, :], compare_op=ALU.not_equal, fill=1.0, base=0,
                                    pattern=[[-1, P]], channel_multiplier=1).then_inc(s_const, 1)
            nc.gpsimd.affine_select(out=causal[:, :], in_=causal[:, :], compare_op=ALU.is_ge, fill=0.0, base=0,
                                    pattern=[[1, P]], channel_multiplier=-1).then_inc(s_const, 1)
            pool.wait_ge(s_const, 8)

            def inverse_std(n, t):
                pool.wait_ge(s_mv[n], t + 1)
                nc.gpsimd.tensor_tensor(var_eps[:, n:n + 1], mv[:, n, 1:2], ln_eps[:, :], ALU.add).then_inc(s_veps[n], 1)
                pool.wait_ge(s_veps[n], t + 1)
                nc.gpsimd.tensor_tensor(rstd[:, n:n + 1], var_eps[:, n:n + 1], minus_half[:, :], ALU.pow).then_inc(s_rstd[n], 1)

            def body(a, f, g):
                if a is not None:
                    inverse_std(LN_X, a)
                if f is not None:
                    pool.wait_ge(s_sc, f + 1)
                    for h in range(HEADS):
                        wait(pool, s_sel, HEADS * f - HEADS + h + 1)
                        wait(pool, s_prob, HEADS * f - HEADS + h + 1)
                        nc.gpsimd.tensor_tensor(
                            sums[:, h, :, :],
                            scores[:, h, 0:XIN].unsqueeze(2).broadcast_to([P, XIN, NKEYS]),
                            scores[:, HEADS + h, :].unsqueeze(1).broadcast_to([P, XIN, NKEYS]),
                            ALU.add).then_inc(s_sum, 1)
                if a is not None:
                    inverse_std(LN_O, a)
                if g is not None:
                    inverse_std(LN_Y, g)
                if a is not None:
                    inverse_std(LN_M, a)

            pipeline(pool, body)

        @block.tensor
        def _(pe):
            pe.wait_ge(s_const, 8)
            pe.wait_ge(s_w, 16 * LOADS)
            pe.wait_ge(s_mem_x, 16 * (1 + DC))

            def setup_bank(n):
                wait(pe, s_set_sb, n - 7)
                return bank[n % 8]

            for n, (blocks, _) in enumerate(turned):
                b = setup_bank(n)
                for k, w in enumerate(blocks):
                    last = nc.tensor.transpose(b[:, k * P:(k + 1) * P], w, ident[:, :])
                last.then_inc(s_set_ps, 1)
            b = setup_bank(SET_KEYS)
            for side in range(SIDES):
                for h in range(HEADS):
                    g = side * HEADS + h
                    last = nc.tensor.transpose(b[0:KDIM, g * NKEYS:(g + 1) * NKEYS], keys_in[:, h, side, :],
                                               ident[0:NKEYS, 0:NKEYS])
            last.then_inc(s_set_ps, 1)
            pe.wait_ge(s_set_sb, 2)
            for n, lhs in ((SET_WVO, wv_in), (SET_MEM, memT)):
                b = setup_bank(n)
                for dc in range(DC):
                    for mc in range(DC):
                        last = nc.tensor.matmul(b[:, dc * D:(dc + 1) * D], lhs[:, mc, dc * P:(dc + 1) * P], woT[:, mc, :],
                                                start=(mc == 0), stop=(mc == DC - 1))
                last.then_inc(s_set_ps, 1)
            pe.wait_ge(s_set_sb, SET_KEYS + 1)
            for dc in range(DC):
                b = setup_bank(SET_ROUTE + dc)
                for g in range(GROUPS):
                    last = nc.tensor.matmul(b[:, g * NKEYS:(g + 1) * NKEYS], wrq_in[:, g, dc * P:(dc + 1) * P],
                                            keysT[:, g, :], start=True, stop=True)
                last.then_inc(s_set_ps, 1)
            nc.tensor.matmul(setup_bank(SET_GATE)[:, 0:1 + D], ones_row[:, :], row_in[:, :],
                             start=True, stop=True).then_inc(s_set_ps, 1)
            pe.wait_ge(s_set_sb, SET_ALL)
            pe.wait_ge(s_gate, 6)

            def body(a, f, g):
                if f is not None:
                    pe.wait_ge(s_xn2, f + 1)
                    wait(pe, s_xn1T, f + 1)
                    wait(pe, s_sk, f + 1)
                    for c in range(DC):
                        last = nc.tensor.transpose(t_ps[:, c * P:(c + 1) * P], xn2[:, c * P:(c + 1) * P], ident[:, :])
                    last.then_inc(s_xn2T_ps, 1)
                if a is not None:
                    pe.wait_ge(s_xn1, a + 1)
                    wait(pe, s_xn2T, a)
                    for c in range(DC):
                        last = nc.tensor.transpose(t_ps[:, c * P:(c + 1) * P], xn1[:, c * P:(c + 1) * P], ident[:, :])
                    last.then_inc(s_xn1T_ps, 1)
                if f is not None:
                    pe.wait_ge(s_xn2T, f + 1)
                    wait(pe, s_hT, 2 * f)
                    for c in range(DC):
                        last = nc.tensor.matmul(even_ps[:, :], xn2T[:, c, :], route[:, c, :], start=(c == 0), stop=(c == DC - 1))
                    last.then_inc(s_sc_ps, 1)
                    for half in range(2):
                        if half:
                            pe.wait_ge(s_sc, f + 1)
                        for c in range(DC):
                            last = nc.tensor.matmul((odd_ps, even_ps)[half][:, :], xn2T[:, c, :],
                                                    deT[:, c, half * HALF:(half + 1) * HALF],
                                                    start=(c == 0), stop=(c == DC - 1))
                        last.then_inc(s_d_ps, 1)
                if a is not None:
                    pe.wait_ge(s_xn1T, a + 1)
                    wait(pe, s_sig, a)
                    for side, w in enumerate((wqT, wkT)):
                        for ec in range(DC):
                            col = (side * DC + ec) * P
                            for c in range(DC):
                                last = nc.tensor.matmul(qk_ps[:, col:col + P], w[:, c, ec * P:(ec + 1) * P], xn1T[:, c, :],
                                                        start=(c == 0), stop=(c == DC - 1))
                    last.then_inc(s_qk_ps, 1)
                    wait(pe, s_v, a)
                    wait(pe, s_ln_y, a - 2)
                    for c in range(DC):
                        last = nc.tensor.matmul(v_ps, xn1T[:, c, :], wvo[:, c, :], start=(c == 0), stop=(c == DC - 1))
                    last.then_inc(s_v_ps, 1)
                    pe.wait_ge(s_sig, a + 1)
                    wait(pe, s_sk, a)
                    for c in range(DC):
                        last = nc.tensor.transpose(sk_ps[:, c * P:(c + 1) * P], sig[:, DC + c, :], ident[:, :])
                    last.then_inc(s_sk_ps, 1)
                    wait(pe, s_at, a)
                    wait(pe, s_mix_mem, a)
                    for c in range(DC):
                        last = nc.tensor.matmul(at_ps, sig[:, DC + c, :], sig[:, c, :], start=(c == 0), stop=(c == DC - 1))
                    last.then_inc(s_at_ps, 1)
                if g is not None:
                    pe.wait_ge(s_wsum, g + 1)
                    for half in range(2):
                        if f is not None:
                            pe.wait_ge(s_d, 2 * f + 1 + half)
                        for k in range(4):
                            e = 4 * half + k
                            last = nc.tensor.transpose((odd_ps, even_ps)[half][:, k * P:(k + 1) * P],
                                                       wsum[:, e * P:(e + 1) * P], ident[:, :])
                        last.then_inc(s_g_ps, 1)
                if a is not None:
                    b = seq_of(a)
                    pe.wait_ge(s_at, a + 1)
                    for c in range(DC):
                        last = nc.tensor.matmul(mem_ps, sig[:, c, :], mem_x[:, c, :], start=(c == 0), stop=(c == DC - 1))
                    last.then_inc(s_mem_ps, 1)
                    pe.wait_ge(s_state, a + 1)
                    wait(pe, s_mix, a)
                    pe.wait_ge(s_v, a + 1)
                    for c in range(DC):
                        nc.tensor.matmul(num_ps, sig[:, c, :], state[:, b, c, :], start=(c == 0), stop=False)
                    nc.tensor.matmul(num_ps, at[:, :], v_one[:, :], start=False, stop=True).then_inc(s_num_ps, 1)
                    pe.wait_ge(s_sk, a + 1)
                    pe.wait_ge(s_state, BATCH + a)
                    for c in range(DC):
                        last = nc.tensor.matmul(ds_ps[:, c * D:(c + 1) * D], sk_nat[:, c * P:(c + 1) * P], v_one[:, 0:D],
                                                start=True, stop=True)
                    last.then_inc(s_ds_ps, 1)
                if f is not None:
                    for half in range(2):
                        if g is not None:
                            pe.wait_ge(s_gT, 2 * g + 1 + half)
                        else:
                            pe.wait_ge(s_d, 2 * f + 1 + half)
                        for k in range(4):
                            ic = 4 * half + k
                            for c in range(DC):
                                last = nc.tensor.matmul((odd_ps, even_ps)[half][:, k * P:(k + 1) * P],
                                                        wupT[:, c, ic * P:(ic + 1) * P], xn2T[:, c, :],
                                                        start=(c == 0), stop=(c == DC - 1))
                        last.then_inc(s_u_ps, 1)
                if g is not None:
                    pe.wait_ge(s_hT, 2 * g + 2)
                    pe.wait_ge(s_gT, 2 * g + 2)
                    wait(pe, s_ln_y, g)
                    for ic in range(IC):
                        nc.tensor.matmul(y_ps, hT[:, ic, :], wdownT[:, ic, :], start=(ic == 0), stop=False)
                    for e in range(EC):
                        last = nc.tensor.matmul(y_ps, gT[:, e, :], ue[:, e, :], start=False, stop=(e == EC - 1))
                    last.then_inc(s_y_ps, 1)

            pipeline(pe, body)

        @block.scalar
        def _(act):
            for n, (_, dst) in enumerate(turned):
                act.wait_ge(s_set_ps, n + 1)
                nc.scalar.copy(dst, bank[n % 8][:, :]).then_inc(s_set_sb, 1)
            act.wait_ge(s_set_ps, SET_KEYS + 1)
            nc.scalar.copy(keysT[:, :, :], bank[SET_KEYS % 8][0:KDIM, :].rearrange("p (g n) -> p g n", n=NKEYS)).then_inc(s_set_sb, 1)
            act.wait_ge(s_set_ps, SET_WVO + 1)
            nc.scalar.copy(wvo[:, :, :], bank[SET_WVO % 8][:, :].rearrange("p (c n) -> p c n", n=D)).then_inc(s_set_sb, 1)
            act.wait_ge(s_set_ps, SET_MEM + 1)
            nc.scalar.copy(mem_x[:, :, 0:D], bank[SET_MEM % 8][:, :].rearrange("p (c n) -> p c n", n=D)).then_inc(s_set_sb, 1)
            for dc in range(DC):
                act.wait_ge(s_set_ps, SET_ROUTE + dc + 1)
                nc.scalar.copy(route[:, dc, :], bank[(SET_ROUTE + dc) % 8][:, :]).then_inc(s_set_sb, 1)
            act.wait_ge(s_set_ps, SET_GATE + 1)
            nc.scalar.activation(gtmp[:, 0:1], bank[SET_GATE % 8][:, 0:1], ACT.Exp, scale=-1.0).then_inc(s_set_sb, 1)

            def body(a, f, g):
                def up_silu(half):
                    act.wait_ge(s_u_ps, 2 * g + 1 + half)
                    wait(act, s_y_ps, g)
                    nc.scalar.activation(hT[:, 4 * half:4 * half + 4, :].rearrange("p c n -> p (c n)"),
                                         (odd_ps, even_ps)[half][:, :], ACT.Silu).then_inc(s_hT, 1)

                def head_silu(h):
                    act.wait_ge(s_zexp, HEADS * g + h + 1)
                    nc.scalar.activation(wexp[:, h, :], wexp[:, h, :], ACT.Silu).then_inc(s_wexp, 1)

                def down_copy(half):
                    act.wait_ge(s_d_ps, 2 * f + 1 + half)
                    wait(act, s_sel, HEADS * f)
                    wait(act, s_zlast, f)
                    nc.scalar.copy(down[:, half * HALF:(half + 1) * HALF], (odd_ps, even_ps)[half][:, :]).then_inc(s_d, 1)

                def gT_copy(half):
                    act.wait_ge(s_g_ps, 2 * g + 1 + half)
                    wait(act, s_y_ps, g)
                    nc.scalar.copy(gT[:, 4 * half:4 * half + 4, :].rearrange("p c n -> p (c n)"),
                                   (odd_ps, even_ps)[half][:, :]).then_inc(s_gT, 1)

                def head_prob(h):
                    act.wait_ge(s_sum, HEADS * f + h + 1)
                    act.wait_ge(s_negm, f + 1)
                    wait(act, s_zexp, HEADS * f - HEADS + h + 1)
                    nc.scalar.activation(prob[:, h, :], sums[:, h, :, :].rearrange("p x y -> p (x y)"), ACT.Exp,
                                         bias=neg_max[:, h:h + 1]).then_inc(s_prob, 1)

                if f is not None:
                    act.wait_ge(s_xn2T_ps, f + 1)
                    wait(act, s_u_ps, 2 * f)
                    nc.scalar.copy(xn2T[:, :, :].rearrange("p c n -> p (c n)"), t_ps).then_inc(s_xn2T, 1)
                if g is not None:
                    up_silu(0)
                    up_silu(1)
                if a is not None:
                    act.wait_ge(s_xn1T_ps, a + 1)
                    wait(act, s_v_ps, a)
                    nc.scalar.copy(xn1T[:, :, :].rearrange("p c n -> p (c n)"), t_ps).then_inc(s_xn1T, 1)
                if g is not None:
                    head_silu(0)
                if f is not None:
                    act.wait_ge(s_sc_ps, f + 1)
                    wait(act, s_sum, HEADS * f)
                    wait(act, s_xkey, f)
                    nc.scalar.copy(scores[:, :, :].rearrange("p g n -> p (g n)"), even_ps[:, :]).then_inc(s_sc, 1)
                if g is not None:
                    head_silu(1)
                if f is not None:
                    down_copy(0)
                if g is not None:
                    head_silu(2)
                if f is not None:
                    down_copy(1)
                if g is not None:
                    head_silu(3)
                    act.wait_ge(s_zlast, g + 1)
                    wait(act, s_wsum, g)
                    nc.scalar.activation(z_last[:, :], z_last[:, :], ACT.Silu, accum_out=w_last[:, :]).then_inc(s_wlast, 1)
                if a is not None:
                    act.wait_ge(s_qk_ps, a + 1)
                    wait(act, s_sig, a)
                    nc.scalar.activation(eqk[:, :, :].rearrange("p c n -> p (c n)"), qk_ps[:, :], ACT.Exp).then_inc(s_eqk, 1)
                    act.wait_ge(s_v_ps, a + 1)
                    wait(act, s_ds_ps, a)
                    nc.scalar.copy(v_one[:, 0:D], v_ps).then_inc(s_v, 1)
                if f is not None:
                    act.wait_ge(s_cdif, 2 * f + 2)
                    nc.scalar.activation(cdif[:, :], cdif[:, :], ACT.Exp).then_inc(s_cexp, 1)
                if a is not None:
                    act.wait_ge(s_sk_ps, a + 1)
                    wait(act, s_ds_ps, a)
                    nc.scalar.copy(sk_nat[:, :], sk_ps).then_inc(s_sk, 1)
                if f is not None:
                    head_prob(0)
                if g is not None:
                    gT_copy(0)
                if f is not None:
                    head_prob(1)
                if g is not None:
                    gT_copy(1)
                if f is not None:
                    head_prob(2)
                    head_prob(3)

            pipeline(act, body)

        @block.vector
        def _(dve):
            dve.wait_ge(s_set_sb, SET_ALL)
            nc.vector.reduce_sum(gtmp[:, 2:3], bank[SET_GATE % 8][:, 1:1 + D], axis=AX.X).then_inc(s_gate, 1)
            nc.vector.tensor_scalar(gtmp[:, 1:2], gtmp[:, 0:1], 1.0, None, ALU.add).then_inc(s_gate, 1)
            dve.wait_ge(s_gate, 2)
            nc.vector.reciprocal(gtmp[:, 0:1], gtmp[:, 1:2]).then_inc(s_gate, 1)
            nc.vector.tensor_scalar(gtmp[:, 3:4], gtmp[:, 2:3], EPS, None, ALU.is_ge).then_inc(s_gate, 1)
            dve.wait_ge(s_gate, 4)
            nc.vector.tensor_tensor(gates[:, 0:1], gtmp[:, 0:1], gtmp[:, 3:4], ALU.mult).then_inc(s_gate, 1)
            nc.vector.tensor_scalar(gates[:, 1:2], gtmp[:, 0:1], -1.0, 1.0, ALU.mult, ALU.add).then_inc(s_gate, 1)
            dve.wait_ge(s_gate, 6)
            dve.wait_ge(s_const, 8)

            def moments(n, src, t):
                wait(dve, s_mv[n], t)
                alone(dve)
                nc.vector.bn_stats(stats[:, n, :], src).then_inc(s_stats[n], 1)
                dve.wait_ge(s_stats[n], t + 1)
                alone(dve)
                nc.vector.bn_aggr(mv[:, n, :], stats[:, n, :]).then_inc(s_mv[n], 1)

            def normed(n, dst, src, t, done):
                dve.wait_ge(s_rstd[n], t + 1)
                nc.vector.tensor_scalar(dst, src, mv[:, n, 0:1], rstd[:, n:n + 1], ALU.subtract, ALU.mult).then_inc(done, 1)

            def per_head(x, width):
                return x.unsqueeze(2).broadcast_to([P, HEADS, width])

            def body(a, f, g):
                if a is not None:
                    dve.wait_ge(s_x, 16 * (a + 1))
                    wait(dve, s_xn1, a)
                    moments(LN_X, x_in[:, slot(a), :], a)
                if f is not None:
                    wait(dve, s_xn2T_ps, f)
                    normed(LN_M, xn2[:, :], x_mid[:, slot(f), :], f, s_xn2)
                if a is not None:
                    wait(dve, s_xn1T_ps, a)
                    normed(LN_X, xn1[:, :], x_in[:, slot(a), :], a, s_xn1)
                if g is not None:
                    dve.wait_ge(s_wexp, HEADS * g + HEADS)
                    nc.vector.tensor_tensor(wexp[:, 0:2, :], wexp[:, 0:2, :], wexp[:, 2:4, :], ALU.add).then_inc(s_w2, 1)
                    dve.wait_ge(s_w2, g + 1)
                    wait(dve, s_g_ps, 2 * g)
                    nc.vector.tensor_tensor(wsum[:, :], wexp[:, 0, :], wexp[:, 1, :], ALU.add).then_inc(s_w1, 1)
                    dve.wait_ge(s_w1, g + 1)
                    dve.wait_ge(s_wlast, g + 1)
                    nc.vector.tensor_tensor(wsum[:, LAST_IN:], wsum[:, LAST_IN:], w_last[:, :], ALU.add).then_inc(s_wsum, 1)
                if f is not None:
                    dve.wait_ge(s_sc, f + 1)
                    wait(dve, s_cand, f)
                    alone(dve)
                    for n in range(GROUPS):
                        last = nc.vector.max(top[:, n, :], scores[:, n, :])
                    last.then_inc(s_top, 1)
                    dve.wait_ge(s_top, f + 1)
                    wait(dve, s_clamped, f)
                    alone(dve)
                    for h in range(HEADS):
                        last = nc.vector.max_index(x_key[:, h, :], top[:, h, :], scores[:, h, :])
                    last.then_inc(s_xkey, 1)
                    wait(dve, s_cm1, f)
                    nc.vector.tensor_tensor(cand[:, :, :, :],
                                            top[:, 0:HEADS, :].unsqueeze(3).broadcast_to([P, HEADS, TOP, TOP]),
                                            top[:, HEADS:, :].unsqueeze(2).broadcast_to([P, HEADS, TOP, TOP]),
                                            ALU.add).then_inc(s_cand, 1)
                    dve.wait_ge(s_xkey, f + 1)
                    wait(dve, s_cm2, f)
                    nc.vector.tensor_scalar(clamped[:, :, :], x_key[:, :, :], float(XIN), None, ALU.is_ge).then_inc(s_clamped, 1)
                    dve.wait_ge(s_cand, f + 1)
                    wait(dve, s_sel, HEADS * f)
                    alone(dve)
                    for h in range(HEADS):
                        last = nc.vector.max(best[:, h, :], cand[:, h, :, :].rearrange("p x y -> p (x y)"))
                    last.then_inc(s_best, 1)
                    dve.wait_ge(s_best, f + 1)
                    wait(dve, s_prob, HEADS * f)
                    nc.vector.tensor_scalar(neg_max[:, :], best[:, :, 0], -1.0, None, ALU.mult).then_inc(s_negm, 1)
                    flat = cand[:, :, :, :].rearrange("p h x y -> p h (x y)")
                    wait(dve, s_pe, f)
                    wait(dve, s_zsum, f)
                    nc.vector.tensor_tensor(cdif[:, 0:NC].rearrange("p (h n) -> p h n", h=HEADS), flat,
                                            per_head(best[:, :, 0], TOP * TOP), ALU.subtract).then_inc(s_cdif, 1)
                    nc.vector.tensor_tensor(cdif[:, NC:].rearrange("p (h n) -> p h n", h=HEADS), best[:, :, :],
                                            per_head(best[:, :, 0], TOP), ALU.subtract).then_inc(s_cdif, 1)
                    nc.vector.tensor_tensor(cmask[:, :, :, :].rearrange("p h x y -> p h (x y)"), flat,
                                            per_head(best[:, :, TOP - 1], TOP * TOP), ALU.is_ge).then_inc(s_cm1, 1)
                    dve.wait_ge(s_cm1, f + 1)
                    dve.wait_ge(s_clamped, f + 1)
                    nc.vector.tensor_tensor(cmask[:, :, :, :], cmask[:, :, :, :],
                                            clamped[:, :, :].unsqueeze(3).broadcast_to([P, HEADS, TOP, TOP]),
                                            ALU.mult).then_inc(s_cm2, 1)
                if a is not None:
                    dve.wait_ge(s_eqk, a + 1)
                    nc.vector.tensor_scalar(eqk[:, :, :], eqk[:, :, :], 1.0, None, ALU.min).then_inc(s_emin, 1)
                    dve.wait_ge(s_emin, a + 1)
                    wait(dve, s_num_ps, a)
                    dve.wait_ge(s_state, BATCH + a)
                    nc.vector.scalar_tensor_tensor(sig[:, 0:DC, :], qk_ps[:, 0:D].rearrange("p (c n) -> p c n", n=P), 0.0,
                                                   eqk[:, 0:DC, :], ALU.max, ALU.add)
                    for c in range(DC):
                        last = nc.vector.scalar_tensor_tensor(sig[:, DC + c, :], qk_ps[:, D + c * P:D + (c + 1) * P], 0.0,
                                                              eqk[:, DC + c, :], ALU.max, ALU.add,
                                                              accum_out=z_add[:, c:c + 1])
                    last.then_inc(s_sig, 1)
                if f is not None:
                    dve.wait_ge(s_cexp, f + 1)
                    wait(dve, s_rz, f)
                    nc.vector.reduce_sum(zsum[:, :], cdif[:, NC:].rearrange("p (h n) -> p h n", h=HEADS), axis=AX.X).then_inc(s_zsum, 1)
                    dve.wait_ge(s_cm2, f + 1)
                    nc.vector.tensor_tensor(cmask[:, :, :, :].rearrange("p h x y -> p (h x y)"),
                                            cmask[:, :, :, :].rearrange("p h x y -> p (h x y)"), cdif[:, 0:NC],
                                            ALU.mult).then_inc(s_pe, 1)
                    dve.wait_ge(s_zsum, f + 1)
                    wait(dve, s_zexp, HEADS * f)
                    nc.vector.reciprocal(rz[:, :], zsum[:, :]).then_inc(s_rz, 1)
                    dve.wait_ge(s_d, 2 * f + 2)
                    dve.wait_ge(s_rz, f + 1)
                    dve.wait_ge(s_pe, f + 1)
                    wait(dve, s_wlast, f)
                    nc.vector.scalar_tensor_tensor(z_last[:, :].rearrange("p (h n) -> p h n", h=HEADS),
                                                   cmask[:, :, :, :].rearrange("p h x y -> p h (x y)"), down[:, LAST_IN:],
                                                   per_head(rz[:, :], TOP * TOP), ALU.mult, ALU.mult).then_inc(s_zlast, 1)

                    def select(h):
                        dve.wait_ge(s_sum, HEADS * f + h + 1)
                        wait(dve, s_w1, f)
                        nc.vector.scalar_tensor_tensor(wexp[:, h, :], sums[:, h, :, :].rearrange("p x y -> p (x y)"),
                                                       best[:, h, TOP - 1:TOP], down[:, :],
                                                       ALU.is_ge, ALU.mult).then_inc(s_sel, 1)

                    def weigh(h):
                        dve.wait_ge(s_sel, HEADS * f + h + 1)
                        dve.wait_ge(s_prob, HEADS * f + h + 1)
                        nc.vector.scalar_tensor_tensor(wexp[:, h, :], wexp[:, h, :], rz[:, h:h + 1], prob[:, h, :],
                                                       ALU.mult, ALU.mult).then_inc(s_zexp, 1)

                    select(0)
                if a is not None:
                    dve.wait_ge(s_at_ps, a + 1)
                    wait(dve, s_num_ps, a)
                    nc.vector.tensor_tensor(at[:, :], at_ps, causal[:, :], ALU.mult).then_inc(s_at, 1)
                if f is not None:
                    select(1)
                    weigh(0)
                    select(2)
                    weigh(1)
                if a is not None:
                    b = seq_of(a)
                    dve.wait_ge(s_ds_ps, a + 1)
                    dve.wait_ge(s_sig, a + 1)
                    dve.wait_ge(s_state, BATCH + a)
                    nc.vector.tensor_tensor(state[:, b, :, D:D + 1], state[:, b, :, D:D + 1], z_add[:, :].unsqueeze(2), ALU.add)
                    nc.vector.tensor_tensor(state[:, b, :, 0:D], state[:, b, :, 0:D],
                                            ds_ps[:, :].rearrange("p (c n) -> p c n", n=D), ALU.add).then_inc(s_state, 1)
                    dve.wait_ge(s_mem_ps, a + 1)
                    dve.wait_ge(s_num_ps, a + 1)
                    nc.vector.tensor_scalar(dens[:, 0:1], mem_ps[:, D:D + 1], EPS, None, ALU.max).then_inc(s_dens, 1)
                    nc.vector.tensor_scalar(dens[:, 1:2], num_ps[:, D:D + 1], EPS, None, ALU.max).then_inc(s_dens, 1)
                    dve.wait_ge(s_dens, 2 * a + 2)
                    nc.vector.reciprocal(rden[:, :], dens[:, :]).then_inc(s_rden, 1)
                    dve.wait_ge(s_rden, a + 1)
                    nc.vector.tensor_tensor(coef[:, :], rden[:, :], gates[:, :], ALU.mult).then_inc(s_coef, 1)
                    dve.wait_ge(s_coef, a + 1)
                    wait(dve, s_ln_o, a)
                    nc.vector.tensor_scalar(mix[:, :], mem_ps[:, 0:D], coef[:, 0:1], None, ALU.mult).then_inc(s_mix_mem, 1)
                    dve.wait_ge(s_mix_mem, a + 1)
                    nc.vector.scalar_tensor_tensor(mix[:, :], num_ps[:, 0:D], coef[:, 1:2], mix[:, :],
                                                   ALU.mult, ALU.add).then_inc(s_mix, 1)
                    dve.wait_ge(s_mix, a + 1)
                    moments(LN_O, mix[:, :], a)
                if f is not None:
                    select(3)
                    weigh(2)
                if a is not None:
                    wait(dve, s_xmid, a)
                    normed(LN_O, ln_o[:, :], mix[:, :], a, s_ln_o)
                if f is not None:
                    weigh(3)
                if a is not None:
                    dve.wait_ge(s_ln_o, a + 1)
                    wait(dve, s_out, a - SLOTS + 2)
                    nc.vector.tensor_tensor(x_mid[:, slot(a), :], x_in[:, slot(a), :], ln_o[:, :], ALU.add).then_inc(s_xmid, 1)
                    dve.wait_ge(s_xmid, a + 1)
                    wait(dve, s_xn2, a)
                    moments(LN_M, x_mid[:, slot(a), :], a)
                if g is not None:
                    dve.wait_ge(s_y_ps, g + 1)
                    wait(dve, s_ln_y, g)
                    moments(LN_Y, y_ps, g)
                    wait(dve, s_out, g)
                    normed(LN_Y, ln_y[:, :], y_ps, g, s_ln_y)
                    dve.wait_ge(s_ln_y, g + 1)
                    wait(dve, s_stored, 16 * g)
                    nc.vector.tensor_tensor(x_out[:, :], x_mid[:, slot(g), :], ln_y[:, :], ALU.add).then_inc(s_out, 1)

            pipeline(dve, body)


_INS = ["L0_attn_hidden_states", "L0_attn_w_q", "L0_attn_w_k", "L0_attn_w_v", "L0_attn_w_o", "L0_attn_gate",
        "L0_attn_memory", "L0_attn_memory_norm", "L0_ffn_W_up", "L0_ffn_W_down", "L0_ffn_W_q", "L0_ffn_keys",
        "L0_ffn_down_embed", "L0_ffn_up_embed"]


def kernel(**inputs):
    import numpy as _np
    import concourse.bacc as _bacc
    from concourse.bass_utils import run_bass_kernel_spmd as _run

    nc = _bacc.Bacc("TRN2", target_bir_lowering=False, num_devices=1)
    arrays, args = {}, []
    for name in _INS:
        a = _np.ascontiguousarray(inputs[name])
        arrays[f"in_{name}_dram"] = a
        args.append(nc.dram_tensor(f"in_{name}_dram", a.shape, mybir.dt.from_np(a.dtype), kind="ExternalInput").ap())
    shape = inputs["L0_attn_hidden_states"].shape
    args.append(nc.dram_tensor("out_0_dram", shape, mybir.dt.float32, kind="ExternalOutput").ap())
    sandwich_kernel(nc, *args)
    r = _run(nc, [arrays], core_ids=[0])
    return r.results[0]["out_0_dram"]
```

```python
import concourse.bass as bass
from concourse import mybir
from contextlib import ExitStack


def sandwich_kernel(nc, hidden, w_q, w_k, w_v, w_o, gate, memory, memory_norm,
                    W_up, W_down, W_rq, keys, down_embed, up_embed, out):
    fp32 = mybir.dt.float32
    ALU = mybir.AluOpType
    ACT = mybir.ActivationFunctionType
    AX = mybir.AxisListType

    BATCH, SEQ, D = hidden.shape
    P = 128
    DC = D // P
    TILES = BATCH * SEQ // P
    CHUNKS = SEQ // P
    INNER = W_up.shape[0]
    IC = INNER // P
    HEADS, NKEYS, SIDES, KDIM = keys.shape
    GROUPS = SIDES * HEADS
    EXPERTS = down_embed.shape[0]
    EC = EXPERTS // P
    XIN = EXPERTS // NKEYS
    TOP = 8
    HALF = 512
    LAST_IN = EXPERTS - 1
    NEAR, WIDE = 2, 2
    FAR = TOP - NEAR
    NCAND = NEAR * TOP + FAR * WIDE
    LN_EPS = 1e-5
    EPS = 1e-6
    SLOTS = 4

    x_tiles = hidden.rearrange("b (c p) d -> p c b d", p=P)
    out_tiles = out.rearrange("b (c p) d -> p c b d", p=P)

    ctx = ExitStack()
    with ctx:
        def sb(name, shape, dt=fp32):
            return ctx.enter_context(nc.sbuf_tensor(name, shape, dt))

        def sem(name):
            return ctx.enter_context(nc.semaphore(name))

        keys_in = sb("keys_in", [NKEYS, HEADS, SIDES, KDIM])
        row_in = sb("row_in", [1, 1 + D])
        wqT, wkT, woT, memT = (sb(n, [P, DC, D]) for n in ("wqT", "wkT", "woT", "memT"))
        wvo = sb("wvo", [P, DC, D])
        mem_x = sb("mem_x", [P, DC, D + 1])
        wupT = sb("wupT", [P, DC, INNER])
        deT = sb("deT", [P, DC, EXPERTS])
        wdownT = sb("wdownT", [P, IC, D])
        ue = sb("ue", [P, EC, D])
        keysT = sb("keysT", [KDIM, GROUPS, NKEYS])
        route = sb("route", [P, DC, GROUPS * NKEYS])
        ident = sb("ident", [P, P])
        causal = sb("causal", [P, P])
        ones_row = sb("ones_row", [1, P])
        minus_half = sb("minus_half", [P, 1])
        ln_eps = sb("ln_eps", [P, 1])
        gates = sb("gates", [P, 2])
        gtmp = sb("gtmp", [P, 4])

        x_in = sb("x_in", [P, SLOTS, D])
        x_mid = sb("x_mid", [P, SLOTS, D])
        x_out = sb("x_out", [P, D])
        stats = sb("stats", [P, 4, 6])
        mv = sb("mv", [P, 4, 2])
        var_eps = sb("var_eps", [P, 4])
        rstd = sb("rstd", [P, 4])
        xn1, xn2, ln_o, ln_y, mix = (sb(n, [P, D]) for n in ("xn1", "xn2", "ln_o", "ln_y", "mix"))
        xn1T, xn2T = (sb(n, [P, DC, P]) for n in ("xn1T", "xn2T"))
        eqk = sb("eqk", [P, 2 * DC, P])
        rqk = sb("rqk", [P, 2 * DC, P])
        sig = sb("sig", [P, 2 * DC, P])
        z_add = sb("z_add", [P, DC])
        v_one = sb("v_one", [P, D + 1])
        sk_nat = sb("sk_nat", [P, D])
        at = sb("at", [P, P])
        dens = sb("dens", [P, 2])
        rden = sb("rden", [P, 2])
        coef = sb("coef", [P, 2])
        state = sb("state", [P, BATCH, DC, D + 1])
        scores = sb("scores", [P, GROUPS, NKEYS])
        top = sb("top", [P, GROUPS, TOP])
        x_key = sb("x_key", [P, HEADS, TOP], mybir.dt.uint32)
        clamped = sb("clamped", [P, HEADS, NCAND])
        cand = sb("cand", [P, HEADS, NCAND])
        best = sb("best", [P, HEADS, TOP])
        neg_max = sb("neg_max", [P, HEADS])
        NC = HEADS * NCAND
        cdif = sb("cdif", [P, NC + HEADS * TOP])
        cmask = sb("cmask", [P, HEADS, NCAND])
        zsum = sb("zsum", [P, HEADS])
        rz = sb("rz", [P, HEADS])
        z_last = sb("z_last", [P, NC])
        w_last = sb("w_last", [P, 1])
        down = sb("down", [P, EXPERTS])
        sums = sb("sums", [P, HEADS, XIN, NKEYS])
        prob = sb("prob", [P, HEADS, EXPERTS])
        zexp = sb("zexp", [P, HEADS, EXPERTS])
        wexp = sb("wexp", [P, HEADS, EXPERTS])
        hT = sb("hT", [P, IC, P])
        gT = sb("gT", [P, EC, P])

        wq_in, wk_in, wv_in, wo_in, mem_in = (
            sums[:, :, :, :].rearrange("p h x y -> p (h x y)")[:, n * DC * D:(n + 1) * DC * D].rearrange("p (c n) -> p c n", n=D)
            for n in range(5))
        wup_in = wexp[:, 0:2, :].rearrange("p h n -> p (h n)").rearrange("p (c n) -> p c n", n=D)
        wdown_in = wexp[:, 2:4, :].rearrange("p h n -> p (h n)").rearrange("p (c n) -> p c n", n=INNER)
        de_in = prob[:, 0:2, :].rearrange("p h n -> p (h n)").rearrange("p (c n) -> p c n", n=D)
        wrq_in = prob[0:KDIM, 2:4, :].rearrange("p h n -> p (h n)").rearrange("p (c n) -> p c n", n=D)

        bank = [ctx.enter_context(nc.psum_tensor(f"bank{n}", [P, HALF], fp32)) for n in range(8)]
        t_ps = bank[0][:, 0:D]
        sk_ps = bank[0][:, D:2 * D]
        qk_ps = ds_ps = bank[1]
        y_ps = bank[2][:, 0:D]
        mem_ps = bank[3][:, 0:D + 1]
        at_ps = bank[3][:, HALF - P:HALF]
        v_ps = bank[4][:, 0:D]
        num_ps = bank[4][:, 0:D + 1]
        sc_ps = bank[5]
        d_ps = (bank[6], bank[7])
        g_ps = (bank[5], bank[6])
        u_ps = (bank[7], bank[5])

        s_w = sem("weights_in")
        s_const = sem("constants_ready")
        s_set_ps = sem("setup_in_psum")
        s_set_sb = sem("setup_evicted")
        s_gate = sem("gate_steps")
        s_passed = sem("waits_passed")
        s_mem_x = sem("memory_norm_in")
        s_x = sem("x_loaded")
        s_stored = sem("x_stored")
        (s_xn1, s_xn1T_ps, s_xn1T, s_qk_ps, s_eqk, s_rqk, s_sig, s_v_ps, s_v, s_sk_ps, s_sk, s_at_ps, s_at,
         s_mem_ps, s_num_ps, s_ds_ps, s_state, s_dens, s_rden, s_coef, s_mix_mem, s_mix, s_ln_o, s_xmid) = (
            sem(n) for n in (
                "xn1_ready", "xn1T_in_psum", "xn1T_ready", "qk_in_psum", "exp_qk_ready", "relu_qk_ready", "sigma_ready",
                "v_in_psum", "v_ready", "sk_in_psum", "sk_ready", "scores_in_psum", "scores_masked", "mem_in_psum",
                "num_in_psum", "state_add_in_psum", "state_ready", "denominators", "denominators_inverted",
                "coefficients", "mix_memory_part", "mix_ready", "mix_normed", "x_mid_ready"))
        (s_xn2, s_xn2T_ps, s_xn2T, s_sc_ps, s_sc, s_top, s_xkey, s_clamped, s_cand, s_best, s_negm, s_cdif, s_cexp,
         s_cm1, s_cm2, s_zsum, s_rz, s_pe, s_zlast, s_d_ps, s_d, s_sum, s_prob, s_sel, s_zexp, s_u_ps) = (
            sem(n) for n in (
                "xn2_ready", "xn2T_in_psum", "xn2T_ready", "route_scores_in_psum", "route_scores_ready", "top_keys",
                "x_key_ready", "clamped_ready", "candidates_ready", "best_ready", "neg_max_ready", "differences_ready",
                "cand_exp_ready", "cand_mask_best", "cand_mask_clamped", "softmax_sums", "softmax_inverses",
                "cand_prob_ready", "last_expert_in_ready", "down_halves_in_psum", "down_halves_ready",
                "head_sums_ready", "head_probs_ready", "head_selected", "head_inputs_ready", "up_halves_in_psum"))
        (s_hT, s_wexp, s_wlast, s_wadd, s_g_ps, s_gT, s_y_ps, s_ln_y, s_out) = (
            sem(n) for n in (
                "hidden_halves_ready", "head_weights_ready", "last_expert_weight", "last_expert_added",
                "expert_weights_T_in_psum", "expert_weights_T_ready", "y_in_psum",
                "y_normed", "x_out_ready"))
        LN_X, LN_O, LN_M, LN_Y = range(4)
        s_stats = [sem(f"ln_stats_{n}") for n in ("x", "o", "mid", "y")]
        s_mv = [sem(f"ln_moments_{n}") for n in ("x", "o", "mid", "y")]
        s_veps = [sem(f"ln_var_eps_{n}") for n in ("x", "o", "mid", "y")]
        s_rstd = [sem(f"ln_rstd_{n}") for n in ("x", "o", "mid", "y")]

        def wait(eng, s, value):
            if not isinstance(value, int) or value > 0:
                eng.wait_ge(s, value)

        def alone(eng):
            eng.sem_inc(s_passed, 1)

        def pipeline(eng, body):
            body(0, None, None)
            body(1, 0, None)
            body(2, 1, 0)
            with eng.Fori(3, TILES) as i:
                body(i, i - 1, i - 2)
            body(None, TILES - 1, TILES - 2)
            body(None, None, TILES - 1)

        def slot(t):
            return t % SLOTS if isinstance(t, int) else t & (SLOTS - 1)

        def seq_of(t):
            return t % BATCH if isinstance(t, int) else t & (BATCH - 1)

        def chunk_of(t):
            return t // BATCH if isinstance(t, int) else (t >> (BATCH.bit_length() - 1)) & (CHUNKS - 1)

        def square_blocks(w):
            return [w[:, rc, dc * P:(dc + 1) * P] for dc in range(DC) for rc in range(DC)]

        def tall_blocks(w, dc, half):
            return [w[:, rc, dc * P:(dc + 1) * P] for rc in range(4 * half, 4 * half + 4)]

        turned = [(square_blocks(w_in), wT[:, :, :].rearrange("p c n -> p (c n)"))
                  for w_in, wT in ((wo_in, woT), (mem_in, memT), (wq_in, wqT), (wk_in, wkT))]
        for w_in, wT in ((wup_in, wupT), (de_in, deT)):
            turned += [(tall_blocks(w_in, dc, half), wT[:, dc, half * HALF:(half + 1) * HALF])
                       for dc in range(DC) for half in range(2)]
        for pair in range(IC // 2):
            turned.append(([wdown_in[:, dc, ic * P:(ic + 1) * P] for ic in (2 * pair, 2 * pair + 1) for dc in range(DC)],
                           wdownT[:, 2 * pair:2 * pair + 2, :].rearrange("p c n -> p (c n)")))
        TURNED = len(turned)
        SET_KEYS, SET_WVO, SET_MEM, SET_ROUTE, SET_GATE = TURNED, TURNED + 1, TURNED + 2, TURNED + 3, TURNED + 3 + DC
        SET_ALL = SET_GATE + 1
        LOADS = 12

        block = ctx.enter_context(nc.Block())

        @block.sync
        def _(sp):
            for dst, src in ((wo_in, w_o), (mem_in, memory), (wq_in, w_q), (wk_in, w_k), (wv_in, w_v),
                             (wup_in, W_up), (de_in, down_embed), (wdown_in, W_down), (ue, up_embed)):
                sp.dma_start(dst[:, :, :], src.rearrange("(c p) n -> p c n", p=P)).then_inc(s_w, 16)
            sp.dma_start(wrq_in[:, :, :], W_rq.rearrange("(g n) d -> n g d", n=KDIM)).then_inc(s_w, 16)
            sp.dma_start(keys_in[:, :, :, :], keys.rearrange("h k s n -> k h s n")).then_inc(s_w, 16)
            sp.dma_start(row_in[:, 0:1], gate.rearrange("(a n) -> a n", a=1)).then_inc(s_w, 16)
            sp.dma_start(row_in[:, 1:1 + D], memory_norm.rearrange("(a n) -> a n", a=1)).then_inc(s_mem_x, 16)
            for dc in range(DC):
                sp.dma_start(mem_x[:, dc, D:D + 1],
                             memory_norm[dc * P:(dc + 1) * P].rearrange("(p a) -> p a", a=1)).then_inc(s_mem_x, 16)

            def load(t):
                wait(sp, s_xmid, t - SLOTS + 1)
                wait(sp, s_x, 16 * t)
                alone(sp)
                sp.dma_start(x_in[:, slot(t), :], x_tiles[:, chunk_of(t), seq_of(t), :]).then_inc(s_x, 16)

            def store(t):
                sp.wait_ge(s_out, t + 1)
                alone(sp)
                sp.dma_start(out_tiles[:, chunk_of(t), seq_of(t), :], x_out[:, :]).then_inc(s_stored, 16)

            AHEAD = 2
            for t in range(2 + AHEAD):
                load(t)
            with sp.Fori(2, TILES - AHEAD) as i:
                load(i + AHEAD)
                store(i - 2)
            for t in range(TILES - AHEAD - 2, TILES):
                store(t)
            sp.wait_ge(s_stored, 16 * TILES)

        @block.gpsimd
        def _(pool):
            nc.gpsimd.memset(ident[:, :], 0.0).then_inc(s_const, 1)
            nc.gpsimd.memset(causal[:, :], 1.0).then_inc(s_const, 1)
            nc.gpsimd.memset(minus_half[:, :], -0.5).then_inc(s_const, 1)
            nc.gpsimd.memset(ln_eps[:, :], LN_EPS).then_inc(s_const, 1)
            nc.gpsimd.memset(ones_row[:, :], 1.0).then_inc(s_const, 1)
            nc.gpsimd.memset(v_one[:, D:D + 1], 1.0).then_inc(s_const, 1)
            for b in range(BATCH):
                nc.gpsimd.memset(state[:, b, :, :], 0.0).then_inc(s_state, 1)
            pool.wait_ge(s_const, 6)
            nc.gpsimd.affine_select(out=ident[:, :], in_=ident[:, :], compare_op=ALU.not_equal, fill=1.0, base=0,
                                    pattern=[[-1, P]], channel_multiplier=1).then_inc(s_const, 1)
            nc.gpsimd.affine_select(out=causal[:, :], in_=causal[:, :], compare_op=ALU.is_ge, fill=0.0, base=0,
                                    pattern=[[1, P]], channel_multiplier=-1).then_inc(s_const, 1)
            pool.wait_ge(s_const, 8)

            def inverse_std(n, t):
                pool.wait_ge(s_mv[n], t + 1)
                nc.gpsimd.tensor_tensor(var_eps[:, n:n + 1], mv[:, n, 1:2], ln_eps[:, :], ALU.add).then_inc(s_veps[n], 1)
                pool.wait_ge(s_veps[n], t + 1)
                nc.gpsimd.tensor_tensor(rstd[:, n:n + 1], var_eps[:, n:n + 1], minus_half[:, :], ALU.pow).then_inc(s_rstd[n], 1)

            def body(a, f, g):
                if a is not None:
                    inverse_std(LN_X, a)
                if f is not None:
                    pool.wait_ge(s_sc, f + 1)
                    for h in range(HEADS):
                        wait(pool, s_sel, HEADS * f - HEADS + h + 1)
                        wait(pool, s_prob, HEADS * f - HEADS + h + 1)
                        nc.gpsimd.tensor_tensor(
                            sums[:, h, :, :],
                            scores[:, h, 0:XIN].unsqueeze(2).broadcast_to([P, XIN, NKEYS]),
                            scores[:, HEADS + h, :].unsqueeze(1).broadcast_to([P, XIN, NKEYS]),
                            ALU.add).then_inc(s_sum, 1)
                if a is not None:
                    inverse_std(LN_O, a)
                    inverse_std(LN_M, a)
                if g is not None:
                    inverse_std(LN_Y, g)

            pipeline(pool, body)

        @block.tensor
        def _(pe):
            pe.wait_ge(s_const, 8)
            pe.wait_ge(s_w, 16 * LOADS)
            pe.wait_ge(s_mem_x, 16 * (1 + DC))

            def setup_bank(n):
                wait(pe, s_set_sb, n - 7)
                return bank[n % 8]

            for n, (blocks, _) in enumerate(turned):
                b = setup_bank(n)
                for k, w in enumerate(blocks):
                    last = nc.tensor.transpose(b[:, k * P:(k + 1) * P], w, ident[:, :])
                last.then_inc(s_set_ps, 1)
            b = setup_bank(SET_KEYS)
            for side in range(SIDES):
                for h in range(HEADS):
                    g = side * HEADS + h
                    last = nc.tensor.transpose(b[0:KDIM, g * NKEYS:(g + 1) * NKEYS], keys_in[:, h, side, :],
                                               ident[0:NKEYS, 0:NKEYS])
            last.then_inc(s_set_ps, 1)
            pe.wait_ge(s_set_sb, 2)
            for n, lhs in ((SET_WVO, wv_in), (SET_MEM, memT)):
                b = setup_bank(n)
                for dc in range(DC):
                    for mc in range(DC):
                        last = nc.tensor.matmul(b[:, dc * D:(dc + 1) * D], lhs[:, mc, dc * P:(dc + 1) * P], woT[:, mc, :],
                                                start=(mc == 0), stop=(mc == DC - 1))
                last.then_inc(s_set_ps, 1)
            pe.wait_ge(s_set_sb, SET_KEYS + 1)
            for dc in range(DC):
                b = setup_bank(SET_ROUTE + dc)
                for g in range(GROUPS):
                    last = nc.tensor.matmul(b[:, g * NKEYS:(g + 1) * NKEYS], wrq_in[:, g, dc * P:(dc + 1) * P],
                                            keysT[:, g, :], start=True, stop=True)
                last.then_inc(s_set_ps, 1)
            nc.tensor.matmul(setup_bank(SET_GATE)[:, 0:1 + D], ones_row[:, :], row_in[:, :],
                             start=True, stop=True).then_inc(s_set_ps, 1)
            pe.wait_ge(s_set_sb, SET_ALL)
            pe.wait_ge(s_gate, 6)

            def body(a, f, g):
                if f is not None:
                    pe.wait_ge(s_xn2, f + 1)
                    wait(pe, s_xn1T, f + 1)
                    wait(pe, s_sk, f + 1)
                    for c in range(DC):
                        last = nc.tensor.transpose(t_ps[:, c * P:(c + 1) * P], xn2[:, c * P:(c + 1) * P], ident[:, :])
                    last.then_inc(s_xn2T_ps, 1)
                if g is not None:
                    pe.wait_ge(s_hT, 2 * g + 2)
                    wait(pe, s_ln_y, g)
                    for ic in range(IC):
                        nc.tensor.matmul(y_ps, hT[:, ic, :], wdownT[:, ic, :], start=(ic == 0), stop=False)
                if a is not None:
                    pe.wait_ge(s_xn1, a + 1)
                    wait(pe, s_xn2T, a)
                    for c in range(DC):
                        last = nc.tensor.transpose(t_ps[:, c * P:(c + 1) * P], xn1[:, c * P:(c + 1) * P], ident[:, :])
                    last.then_inc(s_xn1T_ps, 1)
                if f is not None:
                    pe.wait_ge(s_xn2T, f + 1)
                    wait(pe, s_hT, 2 * f)
                    for c in range(DC):
                        last = nc.tensor.matmul(sc_ps[:, :], xn2T[:, c, :], route[:, c, :], start=(c == 0), stop=(c == DC - 1))
                    last.then_inc(s_sc_ps, 1)
                    wait(pe, s_gT, 2 * f - 2)
                    for half in range(2):
                        for c in range(DC):
                            last = nc.tensor.matmul(d_ps[half][:, :], xn2T[:, c, :],
                                                    deT[:, c, half * HALF:(half + 1) * HALF],
                                                    start=(c == 0), stop=(c == DC - 1))
                        last.then_inc(s_d_ps, 1)
                if a is not None:
                    pe.wait_ge(s_xn1T, a + 1)
                    wait(pe, s_sig, a)
                    pe.wait_ge(s_state, BATCH + a)
                    for side, w in enumerate((wqT, wkT)):
                        for ec in range(DC):
                            col = (side * DC + ec) * P
                            for c in range(DC):
                                last = nc.tensor.matmul(qk_ps[:, col:col + P], w[:, c, ec * P:(ec + 1) * P], xn1T[:, c, :],
                                                        start=(c == 0), stop=(c == DC - 1))
                    last.then_inc(s_qk_ps, 1)
                    wait(pe, s_v, a)
                    wait(pe, s_mix, a)
                    for c in range(DC):
                        last = nc.tensor.matmul(v_ps, xn1T[:, c, :], wvo[:, c, :], start=(c == 0), stop=(c == DC - 1))
                    last.then_inc(s_v_ps, 1)
                if g is not None:
                    pe.wait_ge(s_wexp, HEADS * g + HEADS)
                    pe.wait_ge(s_wadd, g + 1)
                    wait(pe, s_gT, 2 * g)
                    for half in range(2):
                        if f is not None:
                            pe.wait_ge(*((s_sc, f + 1), (s_d, 2 * f + 1))[half])
                        for k in range(4):
                            e = 4 * half + k
                            for h in range(HEADS):
                                last = nc.tensor.matmul(g_ps[half][:, k * P:(k + 1) * P], wexp[:, h, e * P:(e + 1) * P],
                                                        ident[:, :], is_transpose=True, start=(h == 0), stop=(h == HEADS - 1))
                        last.then_inc(s_g_ps, 1)
                if a is not None:
                    pe.wait_ge(s_sig, a + 1)
                    wait(pe, s_sk, a)
                    for c in range(DC):
                        last = nc.tensor.transpose(sk_ps[:, c * P:(c + 1) * P], sig[:, DC + c, :], ident[:, :])
                    last.then_inc(s_sk_ps, 1)
                    wait(pe, s_at, a)
                    wait(pe, s_mix_mem, a)
                    for c in range(DC):
                        last = nc.tensor.matmul(at_ps, sig[:, DC + c, :], sig[:, c, :], start=(c == 0), stop=(c == DC - 1))
                    last.then_inc(s_at_ps, 1)
                    b = seq_of(a)
                    pe.wait_ge(s_state, a + 1)
                    pe.wait_ge(s_v, a + 1)
                    for c in range(DC):
                        nc.tensor.matmul(num_ps, sig[:, c, :], state[:, b, c, :], start=(c == 0), stop=False)
                    pe.wait_ge(s_at, a + 1)
                    nc.tensor.matmul(num_ps, at[:, :], v_one[:, :], start=False, stop=True).then_inc(s_num_ps, 1)
                    for c in range(DC):
                        last = nc.tensor.matmul(mem_ps, sig[:, c, :], mem_x[:, c, :], start=(c == 0), stop=(c == DC - 1))
                    last.then_inc(s_mem_ps, 1)
                    pe.wait_ge(s_sk, a + 1)
                    for c in range(DC):
                        last = nc.tensor.matmul(ds_ps[:, c * D:(c + 1) * D], sk_nat[:, c * P:(c + 1) * P], v_one[:, 0:D],
                                                start=True, stop=True)
                    last.then_inc(s_ds_ps, 1)
                if g is not None:
                    pe.wait_ge(s_gT, 2 * g + 2)
                    for e in range(EC):
                        last = nc.tensor.matmul(y_ps, gT[:, e, :], ue[:, e, :], start=False, stop=(e == EC - 1))
                    last.then_inc(s_y_ps, 1)
                if f is not None:
                    for half in range(2):
                        if half == 0:
                            pe.wait_ge(s_d, 2 * f + 2)
                        elif g is not None:
                            pe.wait_ge(s_gT, 2 * g + 1)
                        else:
                            pe.wait_ge(s_sc, f + 1)
                        for k in range(4):
                            ic = 4 * half + k
                            for c in range(DC):
                                last = nc.tensor.matmul(u_ps[half][:, k * P:(k + 1) * P],
                                                        wupT[:, c, ic * P:(ic + 1) * P], xn2T[:, c, :],
                                                        start=(c == 0), stop=(c == DC - 1))
                        last.then_inc(s_u_ps, 1)

            pipeline(pe, body)

        @block.scalar
        def _(act):
            for n, (_, dst) in enumerate(turned):
                act.wait_ge(s_set_ps, n + 1)
                nc.scalar.copy(dst, bank[n % 8][:, :]).then_inc(s_set_sb, 1)
            act.wait_ge(s_set_ps, SET_KEYS + 1)
            nc.scalar.copy(keysT[:, :, :], bank[SET_KEYS % 8][0:KDIM, :].rearrange("p (g n) -> p g n", n=NKEYS)).then_inc(s_set_sb, 1)
            act.wait_ge(s_set_ps, SET_WVO + 1)
            nc.scalar.copy(wvo[:, :, :], bank[SET_WVO % 8][:, :].rearrange("p (c n) -> p c n", n=D)).then_inc(s_set_sb, 1)
            act.wait_ge(s_set_ps, SET_MEM + 1)
            nc.scalar.copy(mem_x[:, :, 0:D], bank[SET_MEM % 8][:, :].rearrange("p (c n) -> p c n", n=D)).then_inc(s_set_sb, 1)
            for dc in range(DC):
                act.wait_ge(s_set_ps, SET_ROUTE + dc + 1)
                nc.scalar.copy(route[:, dc, :], bank[(SET_ROUTE + dc) % 8][:, :]).then_inc(s_set_sb, 1)
            act.wait_ge(s_set_ps, SET_GATE + 1)
            nc.scalar.activation(gtmp[:, 0:1], bank[SET_GATE % 8][:, 0:1], ACT.Exp, scale=-1.0).then_inc(s_set_sb, 1)

            def body(a, f, g):
                def up_silu(half):
                    act.wait_ge(s_u_ps, 2 * f + 1 + half)
                    wait(act, s_y_ps, f)
                    nc.scalar.activation(hT[:, 4 * half:4 * half + 4, :].rearrange("p c n -> p (c n)"),
                                         u_ps[half][:, :], ACT.Silu).then_inc(s_hT, 1)

                def head_silu(t, h):
                    act.wait_ge(s_zexp, HEADS * t + h + 1)
                    wait(act, s_g_ps, 2 * t)
                    nc.scalar.activation(wexp[:, h, :], zexp[:, h, :], ACT.Silu).then_inc(s_wexp, 1)

                def down_copy(half):
                    act.wait_ge(s_d_ps, 2 * f + 1 + half)
                    wait(act, s_sel, HEADS * f)
                    wait(act, s_zlast, f)
                    nc.scalar.copy(down[:, half * HALF:(half + 1) * HALF], d_ps[half][:, :]).then_inc(s_d, 1)

                def gT_copy(half):
                    act.wait_ge(s_g_ps, 2 * g + 1 + half)
                    wait(act, s_y_ps, g)
                    nc.scalar.copy(gT[:, 4 * half:4 * half + 4, :].rearrange("p c n -> p (c n)"),
                                   g_ps[half][:, :]).then_inc(s_gT, 1)

                def head_prob(h):
                    act.wait_ge(s_sum, HEADS * f + h + 1)
                    act.wait_ge(s_negm, f + 1)
                    wait(act, s_zexp, HEADS * f - HEADS + h + 1)
                    nc.scalar.activation(prob[:, h, :], sums[:, h, :, :].rearrange("p x y -> p (x y)"), ACT.Exp,
                                         bias=neg_max[:, h:h + 1]).then_inc(s_prob, 1)

                if f is not None:
                    act.wait_ge(s_xn2T_ps, f + 1)
                    wait(act, s_u_ps, 2 * f)
                    nc.scalar.copy(xn2T[:, :, :].rearrange("p c n -> p (c n)"), t_ps).then_inc(s_xn2T, 1)
                if g is not None:
                    head_silu(g, 2)
                if a is not None:
                    act.wait_ge(s_xn1T_ps, a + 1)
                    wait(act, s_v_ps, a)
                    nc.scalar.copy(xn1T[:, :, :].rearrange("p c n -> p (c n)"), t_ps).then_inc(s_xn1T, 1)
                if g is not None:
                    head_silu(g, 3)
                if f is not None:
                    act.wait_ge(s_sc_ps, f + 1)
                    wait(act, s_sum, HEADS * f)
                    wait(act, s_xkey, f)
                    nc.scalar.copy(scores[:, :, :].rearrange("p g n -> p (g n)"), sc_ps[:, :]).then_inc(s_sc, 1)
                    down_copy(0)
                    down_copy(1)
                    act.wait_ge(s_cdif, 2 * f + 2)
                    nc.scalar.activation(cdif[:, :], cdif[:, :], ACT.Exp).then_inc(s_cexp, 1)
                    head_prob(0)
                if a is not None:
                    act.wait_ge(s_qk_ps, a + 1)
                    wait(act, s_sig, a)
                    nc.scalar.activation(eqk[:, :, :].rearrange("p c n -> p (c n)"), qk_ps[:, :], ACT.Exp).then_inc(s_eqk, 1)
                    nc.scalar.activation(rqk[:, :, :].rearrange("p c n -> p (c n)"), qk_ps[:, :], ACT.Relu).then_inc(s_rqk, 1)
                    act.wait_ge(s_v_ps, a + 1)
                    wait(act, s_ds_ps, a)
                    nc.scalar.copy(v_one[:, 0:D], v_ps).then_inc(s_v, 1)
                if f is not None:
                    head_prob(1)
                if g is not None:
                    gT_copy(0)
                if a is not None:
                    act.wait_ge(s_sk_ps, a + 1)
                    wait(act, s_ds_ps, a)
                    nc.scalar.copy(sk_nat[:, :], sk_ps).then_inc(s_sk, 1)
                if g is not None:
                    gT_copy(1)
                if f is not None:
                    head_prob(2)
                    head_prob(3)
                    up_silu(0)
                    up_silu(1)
                    act.wait_ge(s_zlast, f + 1)
                    wait(act, s_wadd, f)
                    nc.scalar.activation(z_last[:, :], z_last[:, :], ACT.Silu, accum_out=w_last[:, :]).then_inc(s_wlast, 1)
                    head_silu(f, 0)
                    head_silu(f, 1)

            pipeline(act, body)

        @block.vector
        def _(dve):
            dve.wait_ge(s_set_sb, SET_ALL)
            nc.vector.reduce_sum(gtmp[:, 2:3], bank[SET_GATE % 8][:, 1:1 + D], axis=AX.X).then_inc(s_gate, 1)
            nc.vector.tensor_scalar(gtmp[:, 1:2], gtmp[:, 0:1], 1.0, None, ALU.add).then_inc(s_gate, 1)
            dve.wait_ge(s_gate, 2)
            nc.vector.reciprocal(gtmp[:, 0:1], gtmp[:, 1:2]).then_inc(s_gate, 1)
            nc.vector.tensor_scalar(gtmp[:, 3:4], gtmp[:, 2:3], EPS, None, ALU.is_ge).then_inc(s_gate, 1)
            dve.wait_ge(s_gate, 4)
            nc.vector.tensor_tensor(gates[:, 0:1], gtmp[:, 0:1], gtmp[:, 3:4], ALU.mult).then_inc(s_gate, 1)
            nc.vector.tensor_scalar(gates[:, 1:2], gtmp[:, 0:1], -1.0, 1.0, ALU.mult, ALU.add).then_inc(s_gate, 1)
            dve.wait_ge(s_gate, 6)
            dve.wait_ge(s_const, 8)

            def moments(n, src, t):
                wait(dve, s_mv[n], t)
                alone(dve)
                nc.vector.bn_stats(stats[:, n, :], src).then_inc(s_stats[n], 1)
                dve.wait_ge(s_stats[n], t + 1)
                alone(dve)
                nc.vector.bn_aggr(mv[:, n, :], stats[:, n, :]).then_inc(s_mv[n], 1)

            def normed(n, dst, src, t, done):
                dve.wait_ge(s_rstd[n], t + 1)
                nc.vector.tensor_scalar(dst, src, mv[:, n, 0:1], rstd[:, n:n + 1], ALU.subtract, ALU.mult).then_inc(done, 1)

            def per_head(x, width):
                return x.unsqueeze(2).broadcast_to([P, HEADS, width])

            def pairs(x, y):
                for a0, na, nb, at0 in ((0, NEAR, TOP, 0), (NEAR, FAR, WIDE, NEAR * TOP)):
                    yield (slice(at0, at0 + na * nb), nb,
                           x[:, :, a0:a0 + na].unsqueeze(3).broadcast_to([P, HEADS, na, nb]),
                           None if y is None else y[:, :, 0:nb].unsqueeze(2).broadcast_to([P, HEADS, na, nb]))

            def select(t, h):
                dve.wait_ge(s_sum, HEADS * t + h + 1)
                dve.wait_ge(s_d, 2 * t + 2)
                wait(dve, s_wexp, HEADS * t - HEADS + h + 1)
                nc.vector.scalar_tensor_tensor(zexp[:, h, :], sums[:, h, :, :].rearrange("p x y -> p (x y)"),
                                               best[:, h, TOP - 1:TOP], down[:, :],
                                               ALU.is_ge, ALU.mult).then_inc(s_sel, 1)

            def weigh(t, h):
                dve.wait_ge(s_sel, HEADS * t + h + 1)
                dve.wait_ge(s_prob, HEADS * t + h + 1)
                nc.vector.scalar_tensor_tensor(zexp[:, h, :], zexp[:, h, :], rz[:, h:h + 1], prob[:, h, :],
                                               ALU.mult, ALU.mult).then_inc(s_zexp, 1)

            def body(a, f, g):
                if f is not None:
                    wait(dve, s_xn2T_ps, f)
                    normed(LN_M, xn2[:, :], x_mid[:, slot(f), :], f, s_xn2)
                if a is not None:
                    dve.wait_ge(s_x, 16 * (a + 1))
                    wait(dve, s_xn1, a)
                    moments(LN_X, x_in[:, slot(a), :], a)
                if g is not None:
                    select(g, 3)
                    weigh(g, 2)
                if a is not None:
                    wait(dve, s_xn1T_ps, a)
                    normed(LN_X, xn1[:, :], x_in[:, slot(a), :], a, s_xn1)
                if g is not None:
                    weigh(g, 3)
                    dve.wait_ge(s_wexp, HEADS * g + 1)
                    dve.wait_ge(s_wlast, g + 1)
                    nc.vector.tensor_tensor(wexp[:, 0, LAST_IN:], wexp[:, 0, LAST_IN:], w_last[:, :], ALU.add).then_inc(s_wadd, 1)
                if f is not None:
                    dve.wait_ge(s_sc, f + 1)
                    wait(dve, s_cand, 2 * f)
                    alone(dve)
                    for n in range(GROUPS):
                        last = nc.vector.max(top[:, n, :], scores[:, n, :])
                    last.then_inc(s_top, 1)
                    dve.wait_ge(s_top, f + 1)
                    wait(dve, s_cm1, f)
                    for cols, nb, x, y in pairs(top[:, 0:HEADS, :], top[:, HEADS:, :]):
                        nc.vector.tensor_tensor(cand[:, :, cols].rearrange("p h (a b) -> p h a b", b=nb), x, y,
                                                ALU.add).then_inc(s_cand, 1)
                    wait(dve, s_clamped, 2 * f)
                    alone(dve)
                    for h in range(HEADS):
                        last = nc.vector.max_index(x_key[:, h, :], top[:, h, :], scores[:, h, :])
                    last.then_inc(s_xkey, 1)
                    dve.wait_ge(s_cand, 2 * f + 2)
                    wait(dve, s_sel, HEADS * f)
                    alone(dve)
                    for h in range(HEADS):
                        last = nc.vector.max(best[:, h, :], cand[:, h, :])
                    last.then_inc(s_best, 1)
                    dve.wait_ge(s_xkey, f + 1)
                    wait(dve, s_cm2, f)
                    for cols, nb, x, _ in pairs(x_key[:, :, :], None):
                        nc.vector.tensor_scalar(clamped[:, :, cols].rearrange("p h (a b) -> p h a b", b=nb), x,
                                                float(XIN), None, ALU.is_ge).then_inc(s_clamped, 1)
                    dve.wait_ge(s_best, f + 1)
                    wait(dve, s_prob, HEADS * f)
                    nc.vector.tensor_scalar(neg_max[:, :], best[:, :, 0], -1.0, None, ALU.mult).then_inc(s_negm, 1)
                    wait(dve, s_pe, f)
                    wait(dve, s_zsum, f)
                    nc.vector.tensor_tensor(cdif[:, 0:NC].rearrange("p (h n) -> p h n", h=HEADS), cand[:, :, :],
                                            per_head(best[:, :, 0], NCAND), ALU.subtract).then_inc(s_cdif, 1)
                    nc.vector.tensor_tensor(cdif[:, NC:].rearrange("p (h n) -> p h n", h=HEADS), best[:, :, :],
                                            per_head(best[:, :, 0], TOP), ALU.subtract).then_inc(s_cdif, 1)
                    nc.vector.tensor_tensor(cmask[:, :, :], cand[:, :, :], per_head(best[:, :, TOP - 1], NCAND),
                                            ALU.is_ge).then_inc(s_cm1, 1)
                    select(f, 0)
                    dve.wait_ge(s_cm1, f + 1)
                    dve.wait_ge(s_clamped, 2 * f + 2)
                    nc.vector.tensor_tensor(cmask[:, :, :], cmask[:, :, :], clamped[:, :, :], ALU.mult).then_inc(s_cm2, 1)
                    dve.wait_ge(s_cexp, f + 1)
                    wait(dve, s_rz, f)
                    nc.vector.reduce_sum(zsum[:, :], cdif[:, NC:].rearrange("p (h n) -> p h n", h=HEADS), axis=AX.X).then_inc(s_zsum, 1)
                    dve.wait_ge(s_cm2, f + 1)
                    nc.vector.tensor_tensor(cmask[:, :, :], cmask[:, :, :],
                                            cdif[:, 0:NC].rearrange("p (h n) -> p h n", h=HEADS), ALU.mult).then_inc(s_pe, 1)
                    dve.wait_ge(s_zsum, f + 1)
                    wait(dve, s_zexp, HEADS * f)
                    nc.vector.reciprocal(rz[:, :], zsum[:, :]).then_inc(s_rz, 1)
                    dve.wait_ge(s_rz, f + 1)
                    dve.wait_ge(s_pe, f + 1)
                    wait(dve, s_wlast, f)
                    nc.vector.scalar_tensor_tensor(z_last[:, :].rearrange("p (h n) -> p h n", h=HEADS),
                                                   cmask[:, :, :], down[:, LAST_IN:],
                                                   per_head(rz[:, :], NCAND), ALU.mult, ALU.mult).then_inc(s_zlast, 1)
                if a is not None:
                    dve.wait_ge(s_eqk, a + 1)
                    dve.wait_ge(s_rqk, a + 1)
                    wait(dve, s_ds_ps, a)
                    dve.wait_ge(s_state, BATCH + a)
                    nc.vector.scalar_tensor_tensor(sig[:, 0:DC, :], eqk[:, 0:DC, :], 1.0, rqk[:, 0:DC, :], ALU.min, ALU.add)
                    for c in range(DC, 2 * DC):
                        last = nc.vector.scalar_tensor_tensor(sig[:, c, :], eqk[:, c, :], 1.0, rqk[:, c, :], ALU.min, ALU.add,
                                                              accum_out=z_add[:, c - DC:c - DC + 1])
                    last.then_inc(s_sig, 1)
                if f is not None:
                    select(f, 1)
                if a is not None:
                    dve.wait_ge(s_at_ps, a + 1)
                    wait(dve, s_num_ps, a)
                    nc.vector.tensor_tensor(at[:, :], at_ps, causal[:, :], ALU.mult).then_inc(s_at, 1)
                if f is not None:
                    weigh(f, 0)
                    select(f, 2)
                if a is not None:
                    dve.wait_ge(s_mem_ps, a + 1)
                    dve.wait_ge(s_num_ps, a + 1)
                    nc.vector.tensor_scalar(dens[:, 0:1], mem_ps[:, D:D + 1], EPS, None, ALU.max).then_inc(s_dens, 1)
                    nc.vector.tensor_scalar(dens[:, 1:2], num_ps[:, D:D + 1], EPS, None, ALU.max).then_inc(s_dens, 1)
                    dve.wait_ge(s_dens, 2 * a + 2)
                    nc.vector.reciprocal(rden[:, :], dens[:, :]).then_inc(s_rden, 1)
                    dve.wait_ge(s_rden, a + 1)
                    nc.vector.tensor_tensor(coef[:, :], rden[:, :], gates[:, :], ALU.mult).then_inc(s_coef, 1)
                    dve.wait_ge(s_coef, a + 1)
                    wait(dve, s_ln_o, a)
                    nc.vector.tensor_scalar(mix[:, :], mem_ps[:, 0:D], coef[:, 0:1], None, ALU.mult).then_inc(s_mix_mem, 1)
                    dve.wait_ge(s_mix_mem, a + 1)
                    nc.vector.scalar_tensor_tensor(mix[:, :], num_ps[:, 0:D], coef[:, 1:2], mix[:, :],
                                                   ALU.mult, ALU.add).then_inc(s_mix, 1)
                    dve.wait_ge(s_mix, a + 1)
                    moments(LN_O, mix[:, :], a)
                    b = seq_of(a)
                    dve.wait_ge(s_ds_ps, a + 1)
                    dve.wait_ge(s_sig, a + 1)
                    dve.wait_ge(s_state, BATCH + a)
                    nc.vector.tensor_tensor(state[:, b, :, D:D + 1], state[:, b, :, D:D + 1], z_add[:, :].unsqueeze(2), ALU.add)
                    nc.vector.tensor_tensor(state[:, b, :, 0:D], state[:, b, :, 0:D],
                                            ds_ps[:, :].rearrange("p (c n) -> p c n", n=D), ALU.add).then_inc(s_state, 1)
                if f is not None:
                    weigh(f, 1)
                if a is not None:
                    wait(dve, s_xmid, a)
                    normed(LN_O, ln_o[:, :], mix[:, :], a, s_ln_o)
                    dve.wait_ge(s_ln_o, a + 1)
                    wait(dve, s_out, a - SLOTS + 2)
                    nc.vector.tensor_tensor(x_mid[:, slot(a), :], x_in[:, slot(a), :], ln_o[:, :], ALU.add).then_inc(s_xmid, 1)
                    dve.wait_ge(s_xmid, a + 1)
                    wait(dve, s_xn2, a)
                    moments(LN_M, x_mid[:, slot(a), :], a)
                if g is not None:
                    dve.wait_ge(s_y_ps, g + 1)
                    wait(dve, s_ln_y, g)
                    moments(LN_Y, y_ps, g)
                    wait(dve, s_out, g)
                    normed(LN_Y, ln_y[:, :], y_ps, g, s_ln_y)
                    dve.wait_ge(s_ln_y, g + 1)
                    wait(dve, s_stored, 16 * g)
                    nc.vector.tensor_tensor(x_out[:, :], x_mid[:, slot(g), :], ln_y[:, :], ALU.add).then_inc(s_out, 1)

            pipeline(dve, body)


_INS = ["L0_attn_hidden_states", "L0_attn_w_q", "L0_attn_w_k", "L0_attn_w_v", "L0_attn_w_o", "L0_attn_gate",
        "L0_attn_memory", "L0_attn_memory_norm", "L0_ffn_W_up", "L0_ffn_W_down", "L0_ffn_W_q", "L0_ffn_keys",
        "L0_ffn_down_embed", "L0_ffn_up_embed"]


def kernel(**inputs):
    import numpy as _np
    import concourse.bacc as _bacc
    from concourse.bass_utils import run_bass_kernel_spmd as _run

    nc = _bacc.Bacc("TRN2", target_bir_lowering=False, num_devices=1)
    arrays, args = {}, []
    for name in _INS:
        a = _np.ascontiguousarray(inputs[name])
        arrays[f"in_{name}_dram"] = a
        args.append(nc.dram_tensor(f"in_{name}_dram", a.shape, mybir.dt.from_np(a.dtype), kind="ExternalInput").ap())
    shape = inputs["L0_attn_hidden_states"].shape
    args.append(nc.dram_tensor("out_0_dram", shape, mybir.dt.float32, kind="ExternalOutput").ap())
    sandwich_kernel(nc, *args)
    r = _run(nc, [arrays], core_ids=[0])
    return r.results[0]["out_0_dram"]
```

```python
import concourse.bass as bass
from concourse import mybir
from contextlib import ExitStack


def sandwich_kernel(nc, hidden, w_q, w_k, w_v, w_o, gate, memory, memory_norm,
                    W_up, W_down, W_rq, keys, down_embed, up_embed, out):
    fp32 = mybir.dt.float32
    fp32r = mybir.dt.float32r
    ALU = mybir.AluOpType
    ACT = mybir.ActivationFunctionType
    AX = mybir.AxisListType

    BATCH, SEQ, D = hidden.shape
    P = 128
    DC = D // P
    TILES = BATCH * SEQ // P
    CHUNKS = SEQ // P
    INNER = W_up.shape[0]
    IC = INNER // P
    HEADS, NKEYS, SIDES, KDIM = keys.shape
    GROUPS = SIDES * HEADS
    EXPERTS = down_embed.shape[0]
    EC = EXPERTS // P
    XIN = EXPERTS // NKEYS
    TOP = 8
    HALF = 512
    LAST_IN = EXPERTS - 1
    NEAR, WIDE = 2, 2
    FAR = TOP - NEAR
    NCAND = NEAR * TOP + FAR * WIDE
    LN_EPS = 1e-5
    EPS = 1e-6
    SLOTS = 4

    x_tiles = hidden.rearrange("b (c p) d -> p c b d", p=P)
    out_tiles = out.rearrange("b (c p) d -> p c b d", p=P)

    ctx = ExitStack()
    with ctx:
        def sb(name, shape, dt=fp32):
            return ctx.enter_context(nc.sbuf_tensor(name, shape, dt))

        def sem(name):
            return ctx.enter_context(nc.semaphore(name))

        HIGH, LOW = range(2)

        def halves(name, shape):
            return sb(name + "_high", shape, fp32r), sb(name + "_low", shape, fp32r)

        wqT, wkT = (sb(n, [P, DC, D]) for n in ("wqT", "wkT"))
        wvo = sb("wvo", [P, DC, D])
        mem_x = sb("mem_x", [P, DC, D + 1])
        wupT = sb("wupT", [P, DC, INNER])
        deT = halves("deT", [P, DC, EXPERTS])
        wdownT = halves("wdownT", [P, IC, D])
        ue = halves("ue", [P, EC, D])
        route = halves("route", [P, DC, GROUPS * NKEYS])
        ident = sb("ident", [P, P])
        causal = sb("causal", [P, P])
        ones_row = sb("ones_row", [1, P])
        minus_half = sb("minus_half", [P, 1])
        ln_eps = sb("ln_eps", [P, 1])
        gates = sb("gates", [P, 2])
        gtmp = sb("gtmp", [P, 4])

        x_in = sb("x_in", [P, SLOTS, D])
        x_mid = sb("x_mid", [P, SLOTS, D])
        x_out = sb("x_out", [P, D])
        stats = sb("stats", [P, 4, 6])
        mv = sb("mv", [P, 4, 2])
        var_eps = sb("var_eps", [P, 4])
        rstd = sb("rstd", [P, 4])
        xn1, xn2, ln_o, ln_y, mix = (sb(n, [P, D]) for n in ("xn1", "xn2", "ln_o", "ln_y", "mix"))
        xn1T, xn2F = (sb(n, [P, DC, P]) for n in ("xn1T", "xn2F"))
        xn2T = halves("xn2T", [P, DC, P])
        eqk = sb("eqk", [P, 2 * DC, P])
        rqk = sb("rqk", [P, 2 * DC, P])
        sig = sb("sig", [P, 2 * DC, P])
        z_add = sb("z_add", [P, DC])
        v_one = sb("v_one", [P, D + 1])
        sk_nat = sb("sk_nat", [P, D])
        at = sb("at", [P, P])
        dens = sb("dens", [P, 2])
        rden = sb("rden", [P, 2])
        coef = sb("coef", [P, 2])
        state = sb("state", [P, BATCH, DC, D + 1])
        scores = sb("scores", [P, GROUPS, NKEYS])
        top = sb("top", [P, GROUPS, TOP])
        x_key = sb("x_key", [P, HEADS, TOP], mybir.dt.uint32)
        clamped = sb("clamped", [P, HEADS, NCAND])
        cand = sb("cand", [P, HEADS, NCAND])
        best = sb("best", [P, HEADS, TOP])
        neg_max = sb("neg_max", [P, HEADS])
        NC = HEADS * NCAND
        cdif = sb("cdif", [P, NC + HEADS * TOP])
        cmask = sb("cmask", [P, HEADS, NCAND])
        zsum = sb("zsum", [P, HEADS])
        rz = sb("rz", [P, HEADS])
        z_last = sb("z_last", [P, NC])
        w_last = sb("w_last", [P, 1])
        down = sb("down", [P, EXPERTS])
        sums = sb("sums", [P, HEADS, XIN, NKEYS])
        prob = sb("prob", [P, HEADS, EXPERTS])
        picked = sb("picked", [P, 2, EXPERTS])
        wexp = sb("wexp", [P, HEADS, EXPERTS])
        y_sb = sb("y_sb", [P, D])
        hF = sb("hF", [P, IC, P])
        hT = halves("hT", [P, IC, P])
        gF = sb("gF", [P, EC, P])
        gT = halves("gT", [P, EC, P])

        wq_in, wk_in, wv_in, wo_in, mem_in, woT, memT = (
            sums[:, :, :, :].rearrange("p h x y -> p (h x y)")[:, n * DC * D:(n + 1) * DC * D].rearrange("p (c n) -> p c n", n=D)
            for n in range(7))
        wup_in = wexp[:, 0:2, :].rearrange("p h n -> p (h n)").rearrange("p (c n) -> p c n", n=D)
        wdown_in = wexp[:, 2:4, :].rearrange("p h n -> p (h n)").rearrange("p (c n) -> p c n", n=INNER)
        keys_in = (sums[0:NKEYS, :, :, :].rearrange("p h x y -> p (h x y)")[:, 7 * DC * D:7 * DC * D + GROUPS * KDIM]
                   .rearrange("p (h s n) -> p h s n", s=SIDES, n=KDIM))
        keysT = scores[0:KDIM, :, :]
        row_in = hF[0:1, :, :].rearrange("p c n -> p (c n)")[:, 0:1 + D]
        ue_in = picked[:, :, :].rearrange("p h n -> p (h n)").rearrange("p (c n) -> p c n", n=D)
        de_in = prob[:, 0:2, :].rearrange("p h n -> p (h n)").rearrange("p (c n) -> p c n", n=D)
        wrq_in = prob[0:KDIM, 2:4, :].rearrange("p h n -> p (h n)").rearrange("p (c n) -> p c n", n=D)

        bank = [ctx.enter_context(nc.psum_tensor(f"bank{n}", [P, HALF], fp32)) for n in range(8)]
        t_ps = bank[0][:, 0:D]
        sk_ps = bank[0][:, D:2 * D]
        qk_ps = ds_ps = bank[1]
        y_ps = bank[2][:, 0:D]
        mem_ps = bank[3][:, 0:D + 1]
        at_ps = bank[3][:, HALF - P:HALF]
        v_ps = bank[4][:, 0:D]
        num_ps = bank[4][:, 0:D + 1]
        sc_ps = bank[5]
        d_ps = (bank[7], bank[6])
        u_ps = (bank[6], bank[7])
        g_ps = (bank[5], bank[6])

        s_w = sem("weights_in")
        s_const = sem("constants_ready")
        s_set_ps = sem("setup_in_psum")
        s_set_sb = sem("setup_evicted")
        s_set_low = sem("setup_low_halves")
        s_gate = sem("gate_steps")
        s_passed = sem("waits_passed")
        s_mem_x = sem("memory_norm_in")
        s_x = sem("x_loaded")
        s_stored = sem("x_stored")
        (s_xn1, s_xn1T_ps, s_xn1T, s_qk_ps, s_eqk, s_rqk, s_sig, s_v_ps, s_v, s_sk_ps, s_sk, s_at_ps, s_at,
         s_mem_ps, s_num_ps, s_ds_ps, s_state, s_dens, s_rden, s_coef, s_mix_mem, s_mix, s_ln_o, s_xmid) = (
            sem(n) for n in (
                "xn1_ready", "xn1T_in_psum", "xn1T_ready", "qk_in_psum", "exp_qk_ready", "relu_qk_ready", "sigma_ready",
                "v_in_psum", "v_ready", "sk_in_psum", "sk_ready", "scores_in_psum", "scores_masked", "mem_in_psum",
                "num_in_psum", "state_add_in_psum", "state_ready", "denominators", "denominators_inverted",
                "coefficients", "mix_memory_part", "mix_ready", "mix_normed", "x_mid_ready"))
        (s_xn2, s_xn2T_ps, s_xn2F, s_xn2T, s_xn2L, s_sc_ps, s_sc, s_top, s_xkey, s_clamped, s_cand, s_best, s_negm, s_cdif, s_cexp,
         s_cm1, s_cm2, s_zsum, s_rz, s_pe, s_zlast, s_d_ps, s_d, s_sum, s_prob, s_sel, s_zexp, s_u_ps) = (
            sem(n) for n in (
                "xn2_ready", "xn2T_in_psum", "xn2T_full_ready", "xn2T_high_ready", "xn2T_low_ready", "route_scores_in_psum", "route_scores_ready", "top_keys",
                "x_key_ready", "clamped_ready", "candidates_ready", "best_ready", "neg_max_ready", "differences_ready",
                "cand_exp_ready", "cand_mask_best", "cand_mask_clamped", "softmax_sums", "softmax_inverses",
                "cand_prob_ready", "last_expert_in_ready", "down_halves_in_psum", "down_halves_ready",
                "head_sums_ready", "head_probs_ready", "head_selected", "head_inputs_ready", "up_halves_in_psum"))
        s_ue = sem("up_embed_split")
        s_hF, s_hL, s_gF, s_gL = (sem(n) for n in (
            "hidden_full_ready", "hidden_low_ready", "expert_weights_T_full_ready", "expert_weights_T_low_ready"))
        (s_hT, s_wexp, s_wlast, s_wadd, s_pair, s_g_ps, s_gT, s_yh, s_y_ps, s_y, s_ln_y, s_out) = (
            sem(n) for n in (
                "hidden_high_ready", "head_weights_ready", "last_expert_weight", "last_expert_added", "head_pairs_summed",
                "expert_weights_T_in_psum", "expert_weights_T_high_ready", "hidden_used", "y_in_psum", "y_ready",
                "y_normed", "x_out_ready"))
        LN_X, LN_O, LN_M, LN_Y = range(4)
        s_stats = [sem(f"ln_stats_{n}") for n in ("x", "o", "mid", "y")]
        s_mv = [sem(f"ln_moments_{n}") for n in ("x", "o", "mid", "y")]
        s_veps = [sem(f"ln_var_eps_{n}") for n in ("x", "o", "mid", "y")]
        s_rstd = [sem(f"ln_rstd_{n}") for n in ("x", "o", "mid", "y")]

        def wait(eng, s, value):
            if not isinstance(value, int) or value > 0:
                eng.wait_ge(s, value)

        def alone(eng):
            eng.sem_inc(s_passed, 1)

        STAGES = 5

        def pipeline(eng, body):
            def peeled(step):
                body(*(t if 0 <= t < TILES else None for t in range(step, step - STAGES, -1)))

            FIRST = STAGES
            for step in range(FIRST):
                peeled(step)
            with eng.Fori(FIRST, TILES) as i:
                body(i, i - 1, i - 2, i - 3, i - 4)
            for step in range(TILES, TILES + STAGES - 1):
                peeled(step)

        def slot(t):
            return t % SLOTS if isinstance(t, int) else t & (SLOTS - 1)

        def seq_of(t):
            return t % BATCH if isinstance(t, int) else t & (BATCH - 1)

        def chunk_of(t):
            return t // BATCH if isinstance(t, int) else (t >> (BATCH.bit_length() - 1)) & (CHUNKS - 1)

        def square_blocks(w):
            return [w[:, rc, dc * P:(dc + 1) * P] for dc in range(DC) for rc in range(DC)]

        def tall_blocks(w, dc, half):
            return [w[:, rc, dc * P:(dc + 1) * P] for rc in range(4 * half, 4 * half + 4)]

        def flat(wT):
            return wT[:, :, :].rearrange("p c n -> p (c n)")

        turned = [(square_blocks(w_in), flat(wT), None)
                  for w_in, wT in ((wo_in, woT), (mem_in, memT), (wq_in, wqT), (wk_in, wkT))]
        parts = [(dc, half, slice(half * HALF, (half + 1) * HALF)) for dc in range(DC) for half in range(2)]
        turned += [(tall_blocks(wup_in, dc, half), wupT[:, dc, cols], None) for dc, half, cols in parts]
        turned += [(tall_blocks(de_in, dc, half), deT[HIGH][:, dc, cols], deT[LOW][:, dc, cols]) for dc, half, cols in parts]
        for pair in range(IC // 2):
            turned.append(([wdown_in[:, dc, ic * P:(ic + 1) * P] for ic in (2 * pair, 2 * pair + 1) for dc in range(DC)],
                           *(w[:, 2 * pair:2 * pair + 2, :].rearrange("p c n -> p (c n)") for w in wdownT)))
        TURNED = len(turned)
        SET_KEYS, SET_WVO, SET_MEM, SET_ROUTE, SET_GATE = TURNED, TURNED + 1, TURNED + 2, TURNED + 3, TURNED + 3 + DC
        SET_ALL = SET_GATE + 1
        split = [(n, high, low) for n, (_, high, low) in enumerate(turned) if low is not None]
        split += [(SET_ROUTE + dc, route[HIGH][:, dc, :], route[LOW][:, dc, :]) for dc in range(DC)]
        split_steps = [n for n, _, _ in split]
        LOADS = 12

        block = ctx.enter_context(nc.Block())

        @block.sync
        def _(sp):
            for dst, src in ((wo_in, w_o), (mem_in, memory), (wq_in, w_q), (wk_in, w_k), (wv_in, w_v),
                             (wup_in, W_up), (de_in, down_embed), (wdown_in, W_down), (ue_in, up_embed)):
                sp.dma_start(dst[:, :, :], src.rearrange("(c p) n -> p c n", p=P)).then_inc(s_w, 16)
            sp.dma_start(wrq_in[:, :, :], W_rq.rearrange("(g n) d -> n g d", n=KDIM)).then_inc(s_w, 16)
            sp.dma_start(keys_in[:, :, :, :], keys.rearrange("h k s n -> k h s n")).then_inc(s_w, 16)
            sp.dma_start(row_in[:, 0:1], gate.rearrange("(a n) -> a n", a=1)).then_inc(s_w, 16)
            sp.dma_start(row_in[:, 1:1 + D], memory_norm.rearrange("(a n) -> a n", a=1)).then_inc(s_mem_x, 16)
            for dc in range(DC):
                sp.dma_start(mem_x[:, dc, D:D + 1],
                             memory_norm[dc * P:(dc + 1) * P].rearrange("(p a) -> p a", a=1)).then_inc(s_mem_x, 16)

            def load(t):
                wait(sp, s_xmid, t - SLOTS + 1)
                alone(sp)
                wait(sp, s_x, 16 * t)
                alone(sp)
                sp.dma_start(x_in[:, slot(t), :], x_tiles[:, chunk_of(t), seq_of(t), :]).then_inc(s_x, 16)

            def store(t):
                sp.wait_ge(s_out, t + 1)
                alone(sp)
                sp.dma_start(out_tiles[:, chunk_of(t), seq_of(t), :], x_out[:, :]).then_inc(s_stored, 16)

            LEAD = STAGES + 1
            for t in range(LEAD):
                load(t)
            with sp.Fori(LEAD, TILES) as i:
                load(i)
                store(i - LEAD)
            for t in range(TILES - LEAD, TILES):
                store(t)
            sp.wait_ge(s_stored, 16 * TILES)

        @block.gpsimd
        def _(pool):
            nc.gpsimd.memset(ident[:, :], 0.0).then_inc(s_const, 1)
            nc.gpsimd.memset(causal[:, :], 1.0).then_inc(s_const, 1)
            nc.gpsimd.memset(minus_half[:, :], -0.5).then_inc(s_const, 1)
            nc.gpsimd.memset(ln_eps[:, :], LN_EPS).then_inc(s_const, 1)
            nc.gpsimd.memset(ones_row[:, :], 1.0).then_inc(s_const, 1)
            nc.gpsimd.memset(v_one[:, D:D + 1], 1.0).then_inc(s_const, 1)
            for b in range(BATCH):
                nc.gpsimd.memset(state[:, b, :, :], 0.0).then_inc(s_state, 1)
            pool.wait_ge(s_const, 6)
            nc.gpsimd.affine_select(out=ident[:, :], in_=ident[:, :], compare_op=ALU.not_equal, fill=1.0, base=0,
                                    pattern=[[-1, P]], channel_multiplier=1).then_inc(s_const, 1)
            nc.gpsimd.affine_select(out=causal[:, :], in_=causal[:, :], compare_op=ALU.is_ge, fill=0.0, base=0,
                                    pattern=[[1, P]], channel_multiplier=-1).then_inc(s_const, 1)
            pool.wait_ge(s_const, 8)
            pool.wait_ge(s_w, 16 * LOADS)
            pool.wait_ge(s_ue, 1)
            nc.gpsimd.tensor_tensor(flat(ue[LOW]), flat(ue_in), flat(ue[HIGH]).bitcast(fp32), ALU.subtract).then_inc(s_ue, 1)

            def inverse_std(n, t):
                pool.wait_ge(s_mv[n], t + 1)
                nc.gpsimd.tensor_tensor(var_eps[:, n:n + 1], mv[:, n, 1:2], ln_eps[:, :], ALU.add).then_inc(s_veps[n], 1)
                pool.wait_ge(s_veps[n], t + 1)
                nc.gpsimd.tensor_tensor(rstd[:, n:n + 1], var_eps[:, n:n + 1], minus_half[:, :], ALU.pow).then_inc(s_rstd[n], 1)

            def low_half(full, high_low, part, s_full, s_high, count, s_used, used, done):
                pool.wait_ge(s_full, count)
                pool.wait_ge(s_high, count)
                wait(pool, s_used, used)
                nc.gpsimd.tensor_tensor(flat(high_low[LOW][:, part, :]), flat(full[:, part, :]),
                                        flat(high_low[HIGH][:, part, :]).bitcast(fp32), ALU.subtract).then_inc(done, 1)

            def of_half(half):
                return slice(4 * half, 4 * half + 4)

            def body(n, a, f, g, h):
                def head_sums(k):
                    pool.wait_ge(s_sc, f + 1)
                    wait(pool, s_sel, HEADS * f - HEADS + k + 1)
                    wait(pool, s_prob, HEADS * f - HEADS + k + 1)
                    nc.gpsimd.tensor_tensor(sums[:, k, :, :],
                                            scores[:, k, 0:XIN].unsqueeze(2).broadcast_to([P, XIN, NKEYS]),
                                            scores[:, HEADS + k, :].unsqueeze(1).broadcast_to([P, XIN, NKEYS]),
                                            ALU.add).then_inc(s_sum, 1)

                def add_pair(k):
                    pool.wait_ge(s_wexp, HEADS * g + 2 * k + 2)
                    nc.gpsimd.tensor_tensor(wexp[:, 2 * k + 1, :], wexp[:, 2 * k, :], wexp[:, 2 * k + 1, :], ALU.add).then_inc(s_pair, 1)

                if f is not None:
                    low_half(xn2F, xn2T, slice(0, DC), s_xn2F, s_xn2T, f + 1, s_d_ps, 2 * f, s_xn2L)
                if h is not None:
                    low_half(gF, gT, of_half(0), s_gF, s_gT, 2 * h + 1, s_y_ps, h, s_gL)
                if g is not None:
                    pool.wait_ge(s_wlast, g + 1)
                    pool.wait_ge(s_wexp, HEADS * g + 1)
                    nc.gpsimd.tensor_tensor(wexp[:, 0, LAST_IN:], wexp[:, 0, LAST_IN:], w_last[:, :], ALU.add).then_inc(s_wadd, 1)
                    pool.wait_ge(s_wadd, g + 1)
                    add_pair(0)
                if h is not None:
                    low_half(gF, gT, of_half(1), s_gF, s_gT, 2 * h + 2, s_y_ps, h, s_gL)
                for k in range(HEADS):
                    if f is not None:
                        head_sums(k)
                    if n is not None and k == 1:
                        inverse_std(LN_X, n)
                if a is not None:
                    inverse_std(LN_O, a)
                if h is not None:
                    inverse_std(LN_Y, h)
                if g is not None:
                    add_pair(1)
                if a is not None:
                    inverse_std(LN_M, a)
                if f is not None:
                    low_half(hF, hT, of_half(0), s_hF, s_hT, 2 * f + 1, s_yh, f, s_hL)
                if f is not None:
                    low_half(hF, hT, of_half(1), s_hF, s_hT, 2 * f + 2, s_yh, f, s_hL)

            pipeline(pool, body)

        @block.tensor
        def _(pe):
            pe.wait_ge(s_const, 8)
            pe.wait_ge(s_w, 16 * LOADS)
            pe.wait_ge(s_mem_x, 16 * (1 + DC))

            def setup_bank(n):
                wait(pe, s_set_sb, n - 7)
                wait(pe, s_set_low, sum(k <= n - 8 for k in split_steps))
                return bank[n % 8]

            for n, (blocks, _, _) in enumerate(turned):
                b = setup_bank(n)
                for k, w in enumerate(blocks):
                    last = nc.tensor.transpose(b[:, k * P:(k + 1) * P], w, ident[:, :])
                last.then_inc(s_set_ps, 1)
            b = setup_bank(SET_KEYS)
            for side in range(SIDES):
                for h in range(HEADS):
                    g = side * HEADS + h
                    last = nc.tensor.transpose(b[0:KDIM, g * NKEYS:(g + 1) * NKEYS], keys_in[:, h, side, :],
                                               ident[0:NKEYS, 0:NKEYS])
            last.then_inc(s_set_ps, 1)
            pe.wait_ge(s_set_sb, 2)
            for n, lhs in ((SET_WVO, wv_in), (SET_MEM, memT)):
                b = setup_bank(n)
                for dc in range(DC):
                    for mc in range(DC):
                        last = nc.tensor.matmul(b[:, dc * D:(dc + 1) * D], lhs[:, mc, dc * P:(dc + 1) * P], woT[:, mc, :],
                                                start=(mc == 0), stop=(mc == DC - 1))
                last.then_inc(s_set_ps, 1)
            pe.wait_ge(s_set_sb, SET_KEYS + 1)
            for dc in range(DC):
                b = setup_bank(SET_ROUTE + dc)
                for g in range(GROUPS):
                    last = nc.tensor.matmul(b[:, g * NKEYS:(g + 1) * NKEYS], wrq_in[:, g, dc * P:(dc + 1) * P],
                                            keysT[:, g, :], start=True, stop=True)
                last.then_inc(s_set_ps, 1)
            nc.tensor.matmul(setup_bank(SET_GATE)[:, 0:1 + D], ones_row[:, :], row_in[:, :],
                             start=True, stop=True).then_inc(s_set_ps, 1)
            pe.wait_ge(s_set_sb, SET_ALL)
            pe.wait_ge(s_set_low, len(split))
            pe.wait_ge(s_gate, 6)

            def halves_product(out, chunks, lhs, rhs, low_ready, start=True, stop=True):
                terms = [(HIGH, HIGH), (HIGH, LOW), (LOW, HIGH)]
                for k, (i, j) in enumerate(terms):
                    if i == LOW:
                        low_ready()
                    for c in range(chunks):
                        last = nc.tensor.matmul(out, lhs(i, c), rhs(j, c), start=(start and k == 0 and c == 0),
                                                stop=(stop and k == len(terms) - 1 and c == chunks - 1))
                return last

            def body(n, a, f, g, h):
                def low2():
                    pe.wait_ge(s_xn2L, f + 1)

                if f is not None:
                    pe.wait_ge(s_xn2, f + 1)
                    if a is not None:
                        pe.wait_ge(s_xn1T, a + 1)
                    pe.wait_ge(s_sk, f + 1)
                    for c in range(DC):
                        last = nc.tensor.transpose(t_ps[:, c * P:(c + 1) * P], xn2[:, c * P:(c + 1) * P], ident[:, :])
                    last.then_inc(s_xn2T_ps, 1)
                if a is not None:
                    pe.wait_ge(s_xn1T, a + 1)
                    wait(pe, s_sig, a)
                    pe.wait_ge(s_state, BATCH + a)
                    for side, w in enumerate((wqT, wkT)):
                        for ec in range(DC):
                            col = (side * DC + ec) * P
                            for c in range(DC):
                                last = nc.tensor.matmul(qk_ps[:, col:col + P], w[:, c, ec * P:(ec + 1) * P], xn1T[:, c, :],
                                                        start=(c == 0), stop=(c == DC - 1))
                    last.then_inc(s_qk_ps, 1)
                if f is not None:
                    pe.wait_ge(s_xn2T, f + 1)
                    wait(pe, s_gT, 2 * f - 3)
                    halves_product(sc_ps[:, :], DC, lambda i, c: xn2T[i][:, c, :], lambda j, c: route[j][:, c, :],
                                   low2).then_inc(s_sc_ps, 1)
                if a is not None:
                    wait(pe, s_v, a)
                    wait(pe, s_mix, a)
                    for c in range(DC):
                        last = nc.tensor.matmul(v_ps, xn1T[:, c, :], wvo[:, c, :], start=(c == 0), stop=(c == DC - 1))
                    last.then_inc(s_v_ps, 1)
                if f is not None:
                    wait(pe, s_hT, 2 * f)
                    for half in range(2):
                        if half == 1:
                            wait(pe, s_gT, 2 * f - 2)
                        halves_product(d_ps[half][:, :], DC, lambda i, c: xn2T[i][:, c, :],
                                       lambda j, c: deT[j][:, c, half * HALF:(half + 1) * HALF],
                                       low2).then_inc(s_d_ps, 1)
                if h is not None:
                    pe.wait_ge(s_gT, 2 * h + 2)
                    if isinstance(h, int) and h == 0:
                        pe.wait_ge(s_ue, 2)
                    halves_product(y_ps, EC, lambda i, c: gT[i][:, c, :], lambda j, c: ue[j][:, c, :],
                                   lambda: pe.wait_ge(s_gL, 2 * h + 2), start=False).then_inc(s_y_ps, 1)
                if a is not None:
                    pe.wait_ge(s_sig, a + 1)
                    wait(pe, s_sk, a)
                    for c in range(DC):
                        last = nc.tensor.transpose(sk_ps[:, c * P:(c + 1) * P], sig[:, DC + c, :], ident[:, :])
                    last.then_inc(s_sk_ps, 1)
                    wait(pe, s_at, a)
                    wait(pe, s_mix_mem, a)
                    for c in range(DC):
                        last = nc.tensor.matmul(at_ps, sig[:, DC + c, :], sig[:, c, :], start=(c == 0), stop=(c == DC - 1))
                    last.then_inc(s_at_ps, 1)
                    b = seq_of(a)
                    pe.wait_ge(s_state, a + 1)
                    pe.wait_ge(s_v, a + 1)
                    for c in range(DC):
                        nc.tensor.matmul(num_ps, sig[:, c, :], state[:, b, c, :], start=(c == 0), stop=False)
                    pe.wait_ge(s_at, a + 1)
                    nc.tensor.matmul(num_ps, at[:, :], v_one[:, :], start=False, stop=True).then_inc(s_num_ps, 1)
                    for c in range(DC):
                        last = nc.tensor.matmul(mem_ps, sig[:, c, :], mem_x[:, c, :], start=(c == 0), stop=(c == DC - 1))
                    last.then_inc(s_mem_ps, 1)
                    pe.wait_ge(s_sk, a + 1)
                    for c in range(DC):
                        last = nc.tensor.matmul(ds_ps[:, c * D:(c + 1) * D], sk_nat[:, c * P:(c + 1) * P], v_one[:, 0:D],
                                                start=True, stop=True)
                    last.then_inc(s_ds_ps, 1)
                if g is not None:
                    wait(pe, s_y, g)
                    pe.wait_ge(s_hT, 2 * g + 2)
                    halves_product(y_ps, IC, lambda i, c: hT[i][:, c, :], lambda j, c: wdownT[j][:, c, :],
                                   lambda: pe.wait_ge(s_hL, 2 * g + 2), stop=False).then_inc(s_yh, 1)
                if n is not None:
                    pe.wait_ge(s_xn1, n + 1)
                    if f is not None:
                        pe.wait_ge(s_xn2F, f + 1)
                    wait(pe, s_xn1T, n)
                    wait(pe, s_sk, n)
                    for c in range(DC):
                        last = nc.tensor.transpose(t_ps[:, c * P:(c + 1) * P], xn1[:, c * P:(c + 1) * P], ident[:, :])
                    last.then_inc(s_xn1T_ps, 1)
                if f is not None:
                    for half in range(2):
                        pe.wait_ge(s_d, 2 * f + 2 - half)
                        pe.wait_ge(s_xn2F, f + 1)
                        for k in range(4):
                            ic = 4 * half + k
                            for c in range(DC):
                                last = nc.tensor.matmul(u_ps[half][:, k * P:(k + 1) * P], wupT[:, c, ic * P:(ic + 1) * P],
                                                        xn2F[:, c, :], start=(c == 0), stop=(c == DC - 1))
                        last.then_inc(s_u_ps, 1)

                if g is not None:
                    pe.wait_ge(s_pair, HEADS // 2 * (g + 1))
                    wait(pe, s_gT, 2 * g)
                    for half in range(2):
                        if f is not None:
                            pe.wait_ge(*((s_sc, f + 1), (s_hT, 2 * f + 1))[half])
                        for k in range(4):
                            e = 4 * half + k
                            for pair in range(0, HEADS, 2):
                                last = nc.tensor.matmul(g_ps[half][:, k * P:(k + 1) * P], wexp[:, pair + 1, e * P:(e + 1) * P],
                                                        ident[:, :], is_transpose=True, start=(pair == 0), stop=(pair == HEADS - 2))
                        last.then_inc(s_g_ps, 1)
            pipeline(pe, body)

        @block.scalar
        def _(act):
            for n, (_, dst, _) in enumerate(turned):
                act.wait_ge(s_set_ps, n + 1)
                nc.scalar.copy(dst, bank[n % 8][:, :]).then_inc(s_set_sb, 1)
            act.wait_ge(s_set_ps, SET_KEYS + 1)
            nc.scalar.copy(keysT[:, :, :], bank[SET_KEYS % 8][0:KDIM, :].rearrange("p (g n) -> p g n", n=NKEYS)).then_inc(s_set_sb, 1)
            act.wait_ge(s_set_ps, SET_WVO + 1)
            nc.scalar.copy(flat(wvo), bank[SET_WVO % 8][:, :]).then_inc(s_set_sb, 1)
            act.wait_ge(s_set_ps, SET_MEM + 1)
            nc.scalar.copy(mem_x[:, :, 0:D], bank[SET_MEM % 8][:, :].rearrange("p (c n) -> p c n", n=D)).then_inc(s_set_sb, 1)
            for dc in range(DC):
                act.wait_ge(s_set_ps, SET_ROUTE + dc + 1)
                nc.scalar.copy(route[HIGH][:, dc, :], bank[(SET_ROUTE + dc) % 8][:, :]).then_inc(s_set_sb, 1)
            act.wait_ge(s_set_ps, SET_GATE + 1)
            nc.scalar.activation(gtmp[:, 0:1], bank[SET_GATE % 8][:, 0:1], ACT.Exp, scale=-1.0).then_inc(s_set_sb, 1)

            act.wait_ge(s_w, 16 * LOADS)
            nc.scalar.copy(flat(ue[HIGH]), flat(ue_in)).then_inc(s_ue, 1)

            def body(n, a, f, g, h):
                def up_silu(half):
                    act.wait_ge(s_u_ps, 2 * f + 1 + half)
                    wait(act, s_hL, 2 * f)
                    nc.scalar.activation(flat(hF[:, 4 * half:4 * half + 4, :]), u_ps[half][:, :], ACT.Silu).then_inc(s_hF, 1)
                    wait(act, s_yh, f)
                    nc.scalar.activation(flat(hT[HIGH][:, 4 * half:4 * half + 4, :]), u_ps[half][:, :], ACT.Silu).then_inc(s_hT, 1)

                def head_silu(t, h):
                    act.wait_ge(s_zexp, HEADS * t + h + 1)
                    if h % 2 == 0:
                        wait(act, s_pair, 2 * t - 1 + h // 2)
                    else:
                        wait(act, s_g_ps, 2 * t)
                    nc.scalar.activation(wexp[:, h, :], prob[:, h, :], ACT.Silu).then_inc(s_wexp, 1)

                def down_copy(half):
                    act.wait_ge(s_d_ps, 2 * f + 1 + half)
                    wait(act, s_sel, HEADS * f)
                    wait(act, s_zlast, f)
                    nc.scalar.copy(down[:, half * HALF:(half + 1) * HALF], d_ps[half][:, :]).then_inc(s_d, 1)

                def gT_copy(t, half):
                    act.wait_ge(s_g_ps, 2 * t + 1 + half)
                    wait(act, s_gL, 2 * t)
                    nc.scalar.copy(flat(gF[:, 4 * half:4 * half + 4, :]), g_ps[half][:, :]).then_inc(s_gF, 1)
                    wait(act, s_y_ps, t)
                    nc.scalar.copy(flat(gT[HIGH][:, 4 * half:4 * half + 4, :]), g_ps[half][:, :]).then_inc(s_gT, 1)

                def head_prob(h):
                    act.wait_ge(s_sum, HEADS * f + h + 1)
                    act.wait_ge(s_negm, f + 1)
                    wait(act, s_wexp, HEADS * f - HEADS + h + 1)
                    nc.scalar.activation(prob[:, h, :], sums[:, h, :, :].rearrange("p x y -> p (x y)"), ACT.Exp,
                                         bias=neg_max[:, h:h + 1]).then_inc(s_prob, 1)

                if f is not None:
                    act.wait_ge(s_xn2T_ps, f + 1)
                    wait(act, s_u_ps, 2 * f)
                    wait(act, s_xn2L, f)
                    nc.scalar.copy(flat(xn2T[HIGH]), t_ps).then_inc(s_xn2T, 1)
                    nc.scalar.copy(flat(xn2F), t_ps).then_inc(s_xn2F, 1)
                if g is not None:
                    head_silu(g, 1)
                if h is not None:
                    gT_copy(h, 1)
                if a is not None:
                    act.wait_ge(s_qk_ps, a + 1)
                    wait(act, s_sig, a)
                    nc.scalar.activation(rqk[:, :, :].rearrange("p c n -> p (c n)"), qk_ps[:, :], ACT.Relu).then_inc(s_rqk, 1)
                if f is not None:
                    act.wait_ge(s_sc_ps, f + 1)
                    wait(act, s_sum, HEADS * f)
                    wait(act, s_xkey, f)
                    nc.scalar.copy(scores[:, :, :].rearrange("p g n -> p (g n)"), sc_ps[:, :]).then_inc(s_sc, 1)
                if g is not None:
                    head_silu(g, 2)
                    head_silu(g, 3)
                if a is not None:
                    act.wait_ge(s_qk_ps, a + 1)
                    nc.scalar.activation(eqk[:, :, :].rearrange("p c n -> p (c n)"), qk_ps[:, :], ACT.Exp).then_inc(s_eqk, 1)
                if f is not None:
                    act.wait_ge(s_cdif, 2 * f + 2)
                    nc.scalar.activation(cdif[:, :], cdif[:, :], ACT.Exp).then_inc(s_cexp, 1)
                if a is not None:
                    act.wait_ge(s_v_ps, a + 1)
                    wait(act, s_ds_ps, a)
                    nc.scalar.copy(v_one[:, 0:D], v_ps).then_inc(s_v, 1)
                if f is not None:
                    down_copy(0)
                    down_copy(1)
                    head_prob(0)
                if h is not None:
                    act.wait_ge(s_y_ps, h + 1)
                    wait(act, s_ln_y, h)
                    nc.scalar.copy(y_sb[:, :], y_ps).then_inc(s_y, 1)

                if a is not None:
                    act.wait_ge(s_sk_ps, a + 1)
                    wait(act, s_ds_ps, a)
                    nc.scalar.copy(sk_nat[:, :], sk_ps).then_inc(s_sk, 1)
                if f is not None:
                    head_prob(1)
                    head_prob(2)
                    head_prob(3)
                if n is not None:
                    act.wait_ge(s_xn1T_ps, n + 1)
                    wait(act, s_v_ps, n)
                    nc.scalar.copy(flat(xn1T), t_ps).then_inc(s_xn1T, 1)
                if f is not None:
                    up_silu(0)
                    act.wait_ge(s_zlast, f + 1)
                    wait(act, s_wadd, f)
                    nc.scalar.activation(z_last[:, :], z_last[:, :], ACT.Silu, accum_out=w_last[:, :]).then_inc(s_wlast, 1)
                    head_silu(f, 0)
                    up_silu(1)
                if g is not None:
                    gT_copy(g, 0)

            pipeline(act, body)

        @block.vector
        def _(dve):
            for k, (n, high, low) in enumerate(split):
                dve.wait_ge(s_set_sb, n + 1)
                nc.vector.tensor_tensor(low, bank[n % 8][:, :], high.bitcast(fp32), ALU.subtract).then_inc(s_set_low, 1)
            dve.wait_ge(s_set_sb, SET_ALL)
            nc.vector.reduce_sum(gtmp[:, 2:3], bank[SET_GATE % 8][:, 1:1 + D], axis=AX.X).then_inc(s_gate, 1)
            nc.vector.tensor_scalar(gtmp[:, 1:2], gtmp[:, 0:1], 1.0, None, ALU.add).then_inc(s_gate, 1)
            dve.wait_ge(s_gate, 2)
            nc.vector.reciprocal(gtmp[:, 0:1], gtmp[:, 1:2]).then_inc(s_gate, 1)
            nc.vector.tensor_scalar(gtmp[:, 3:4], gtmp[:, 2:3], EPS, None, ALU.is_ge).then_inc(s_gate, 1)
            dve.wait_ge(s_gate, 4)
            nc.vector.tensor_tensor(gates[:, 0:1], gtmp[:, 0:1], gtmp[:, 3:4], ALU.mult).then_inc(s_gate, 1)
            nc.vector.tensor_scalar(gates[:, 1:2], gtmp[:, 0:1], -1.0, 1.0, ALU.mult, ALU.add).then_inc(s_gate, 1)
            dve.wait_ge(s_gate, 6)
            dve.wait_ge(s_const, 8)

            def sums_of_row(n, src, t):
                wait(dve, s_mv[n], t)
                alone(dve)
                nc.vector.bn_stats(stats[:, n, :], src).then_inc(s_stats[n], 1)

            def moments(n, t):
                dve.wait_ge(s_stats[n], t + 1)
                alone(dve)
                nc.vector.bn_aggr(mv[:, n, :], stats[:, n, :]).then_inc(s_mv[n], 1)

            def normed(n, dst, src, t, done):
                dve.wait_ge(s_rstd[n], t + 1)
                nc.vector.tensor_scalar(dst, src, mv[:, n, 0:1], rstd[:, n:n + 1], ALU.subtract, ALU.mult).then_inc(done, 1)

            def per_head(x, width):
                return x.unsqueeze(2).broadcast_to([P, HEADS, width])

            def pairs(x, y):
                for a0, na, nb, at0 in ((0, NEAR, TOP, 0), (NEAR, FAR, WIDE, NEAR * TOP)):
                    yield (slice(at0, at0 + na * nb), nb,
                           x[:, :, a0:a0 + na].unsqueeze(3).broadcast_to([P, HEADS, na, nb]),
                           None if y is None else y[:, :, 0:nb].unsqueeze(2).broadcast_to([P, HEADS, na, nb]))

            def select(t, h):
                if isinstance(t, int) and t == 0:
                    dve.wait_ge(s_ue, 2)
                dve.wait_ge(s_sum, HEADS * t + h + 1)
                dve.wait_ge(s_d, 2 * t + 2)
                wait(dve, s_zexp, HEADS * t + h - 1)
                nc.vector.scalar_tensor_tensor(picked[:, h % 2, :], sums[:, h, :, :].rearrange("p x y -> p (x y)"),
                                               best[:, h, TOP - 1:TOP], down[:, :],
                                               ALU.is_ge, ALU.mult).then_inc(s_sel, 1)

            def weigh(t, h):
                dve.wait_ge(s_sel, HEADS * t + h + 1)
                dve.wait_ge(s_prob, HEADS * t + h + 1)
                nc.vector.scalar_tensor_tensor(prob[:, h, :], picked[:, h % 2, :], rz[:, h:h + 1], prob[:, h, :],
                                               ALU.mult, ALU.mult).then_inc(s_zexp, 1)

            def body(n, a, f, g, h):
                if g is not None:
                    select(g, 3)
                if g is not None:
                    weigh(g, 2)
                if g is not None:
                    weigh(g, 3)
                if f is not None:
                    dve.wait_ge(s_sc, f + 1)
                    wait(dve, s_cand, 2 * f)
                    alone(dve)
                    for k in range(GROUPS):
                        last = nc.vector.max(top[:, k, :], scores[:, k, :])
                    last.then_inc(s_top, 1)
                    dve.wait_ge(s_top, f + 1)
                    wait(dve, s_cm1, f)
                    for cols, nb, x, y in pairs(top[:, 0:HEADS, :], top[:, HEADS:, :]):
                        nc.vector.tensor_tensor(cand[:, :, cols].rearrange("p h (a b) -> p h a b", b=nb), x, y,
                                                ALU.add).then_inc(s_cand, 1)
                    wait(dve, s_clamped, 2 * f)
                    alone(dve)
                    for k in range(HEADS):
                        last = nc.vector.max_index(x_key[:, k, :], top[:, k, :], scores[:, k, :])
                    last.then_inc(s_xkey, 1)
                    dve.wait_ge(s_cand, 2 * f + 2)
                    wait(dve, s_sel, HEADS * f)
                    alone(dve)
                    for k in range(HEADS):
                        last = nc.vector.max(best[:, k, :], cand[:, k, :])
                    last.then_inc(s_best, 1)
                    dve.wait_ge(s_xkey, f + 1)
                    wait(dve, s_cm2, f)
                    for cols, nb, x, _ in pairs(x_key[:, :, :], None):
                        nc.vector.tensor_scalar(clamped[:, :, cols].rearrange("p h (a b) -> p h a b", b=nb), x,
                                                float(XIN), None, ALU.is_ge).then_inc(s_clamped, 1)
                    dve.wait_ge(s_best, f + 1)
                    wait(dve, s_prob, HEADS * f)
                    nc.vector.tensor_scalar(neg_max[:, :], best[:, :, 0], -1.0, None, ALU.mult).then_inc(s_negm, 1)
                    wait(dve, s_pe, f)
                    wait(dve, s_zsum, f)
                    nc.vector.tensor_tensor(cdif[:, 0:NC].rearrange("p (h n) -> p h n", h=HEADS), cand[:, :, :],
                                            per_head(best[:, :, 0], NCAND), ALU.subtract).then_inc(s_cdif, 1)
                    nc.vector.tensor_tensor(cdif[:, NC:].rearrange("p (h n) -> p h n", h=HEADS), best[:, :, :],
                                            per_head(best[:, :, 0], TOP), ALU.subtract).then_inc(s_cdif, 1)
                    nc.vector.tensor_tensor(cmask[:, :, :], cand[:, :, :], per_head(best[:, :, TOP - 1], NCAND),
                                            ALU.is_ge).then_inc(s_cm1, 1)
                if n is not None:
                    dve.wait_ge(s_x, 16 * (n + 1))
                    wait(dve, s_xn1, n)
                    sums_of_row(LN_X, x_in[:, slot(n), :], n)
                if a is not None:
                    dve.wait_ge(s_eqk, a + 1)
                    dve.wait_ge(s_rqk, a + 1)
                    wait(dve, s_ds_ps, a)
                    dve.wait_ge(s_state, BATCH + a)
                    nc.vector.scalar_tensor_tensor(sig[:, 0:DC, :], eqk[:, 0:DC, :], 1.0, rqk[:, 0:DC, :], ALU.min, ALU.add)
                    for c in range(DC, 2 * DC):
                        last = nc.vector.scalar_tensor_tensor(sig[:, c, :], eqk[:, c, :], 1.0, rqk[:, c, :], ALU.min, ALU.add,
                                                              accum_out=z_add[:, c - DC:c - DC + 1])
                    last.then_inc(s_sig, 1)
                if n is not None:
                    moments(LN_X, n)
                if f is not None:
                    dve.wait_ge(s_cm1, f + 1)
                    dve.wait_ge(s_clamped, 2 * f + 2)
                    nc.vector.tensor_tensor(cmask[:, :, :], cmask[:, :, :], clamped[:, :, :], ALU.mult).then_inc(s_cm2, 1)
                    dve.wait_ge(s_cexp, f + 1)
                    wait(dve, s_rz, f)
                    nc.vector.reduce_sum(zsum[:, :], cdif[:, NC:].rearrange("p (h n) -> p h n", h=HEADS), axis=AX.X).then_inc(s_zsum, 1)
                    dve.wait_ge(s_cm2, f + 1)
                    nc.vector.tensor_tensor(cmask[:, :, :], cmask[:, :, :],
                                            cdif[:, 0:NC].rearrange("p (h n) -> p h n", h=HEADS), ALU.mult).then_inc(s_pe, 1)
                if a is not None:
                    dve.wait_ge(s_at_ps, a + 1)
                    wait(dve, s_num_ps, a)
                    nc.vector.tensor_tensor(at[:, :], at_ps, causal[:, :], ALU.mult).then_inc(s_at, 1)
                if f is not None:
                    select(f, 0)
                    select(f, 1)
                if a is not None:
                    dve.wait_ge(s_mem_ps, a + 1)
                    dve.wait_ge(s_num_ps, a + 1)
                    nc.vector.tensor_scalar(dens[:, 0:1], mem_ps[:, D:D + 1], EPS, None, ALU.max).then_inc(s_dens, 1)
                    nc.vector.tensor_scalar(dens[:, 1:2], num_ps[:, D:D + 1], EPS, None, ALU.max).then_inc(s_dens, 1)
                if f is not None:
                    dve.wait_ge(s_zsum, f + 1)
                    wait(dve, s_zexp, HEADS * f)
                    nc.vector.reciprocal(rz[:, :], zsum[:, :]).then_inc(s_rz, 1)
                if a is not None:
                    dve.wait_ge(s_dens, 2 * a + 2)
                    nc.vector.reciprocal(rden[:, :], dens[:, :]).then_inc(s_rden, 1)
                if f is not None:
                    dve.wait_ge(s_rz, f + 1)
                    dve.wait_ge(s_pe, f + 1)
                    wait(dve, s_wlast, f)
                    nc.vector.scalar_tensor_tensor(z_last[:, :].rearrange("p (h n) -> p h n", h=HEADS),
                                                   cmask[:, :, :], down[:, LAST_IN:],
                                                   per_head(rz[:, :], NCAND), ALU.mult, ALU.mult).then_inc(s_zlast, 1)
                if a is not None:
                    dve.wait_ge(s_rden, a + 1)
                    nc.vector.tensor_tensor(coef[:, :], rden[:, :], gates[:, :], ALU.mult).then_inc(s_coef, 1)
                if h is not None:
                    dve.wait_ge(s_y, h + 1)
                    wait(dve, s_ln_y, h)
                    sums_of_row(LN_Y, y_sb[:, :], h)
                if a is not None:
                    dve.wait_ge(s_coef, a + 1)
                    wait(dve, s_ln_o, a)
                    nc.vector.tensor_scalar(mix[:, :], mem_ps[:, 0:D], coef[:, 0:1], None, ALU.mult).then_inc(s_mix_mem, 1)
                if h is not None:
                    moments(LN_Y, h)
                if a is not None:
                    dve.wait_ge(s_mix_mem, a + 1)
                    nc.vector.scalar_tensor_tensor(mix[:, :], num_ps[:, 0:D], coef[:, 1:2], mix[:, :],
                                                   ALU.mult, ALU.add).then_inc(s_mix, 1)
                if n is not None:
                    wait(dve, s_xn1T_ps, n)
                    normed(LN_X, xn1[:, :], x_in[:, slot(n), :], n, s_xn1)
                if a is not None:
                    dve.wait_ge(s_mix, a + 1)
                    sums_of_row(LN_O, mix[:, :], a)
                if a is not None:
                    moments(LN_O, a)
                if f is not None:
                    weigh(f, 0)
                if a is not None:
                    wait(dve, s_xmid, a)
                    normed(LN_O, ln_o[:, :], mix[:, :], a, s_ln_o)
                    b = seq_of(a)
                    dve.wait_ge(s_ds_ps, a + 1)
                    dve.wait_ge(s_sig, a + 1)
                    dve.wait_ge(s_state, BATCH + a)
                    nc.vector.tensor_tensor(state[:, b, :, D:D + 1], state[:, b, :, D:D + 1], z_add[:, :].unsqueeze(2), ALU.add)
                    nc.vector.tensor_tensor(state[:, b, :, 0:D], state[:, b, :, 0:D],
                                            ds_ps[:, :].rearrange("p (c n) -> p c n", n=D), ALU.add).then_inc(s_state, 1)
                    dve.wait_ge(s_ln_o, a + 1)
                    wait(dve, s_out, a - SLOTS + 1)
                    nc.vector.tensor_tensor(x_mid[:, slot(a), :], x_in[:, slot(a), :], ln_o[:, :], ALU.add).then_inc(s_xmid, 1)
                if h is not None:
                    wait(dve, s_out, h)
                    normed(LN_Y, ln_y[:, :], y_sb[:, :], h, s_ln_y)
                if a is not None:
                    dve.wait_ge(s_xmid, a + 1)
                    wait(dve, s_xn2, a)
                    sums_of_row(LN_M, x_mid[:, slot(a), :], a)
                if h is not None:
                    dve.wait_ge(s_ln_y, h + 1)
                    wait(dve, s_stored, 16 * h)
                    nc.vector.tensor_tensor(x_out[:, :], x_mid[:, slot(h), :], ln_y[:, :], ALU.add).then_inc(s_out, 1)
                if a is not None:
                    moments(LN_M, a)
                if f is not None:
                    weigh(f, 1)
                if a is not None:
                    wait(dve, s_xn2T_ps, a)
                    normed(LN_M, xn2[:, :], x_mid[:, slot(a), :], a, s_xn2)
                if f is not None:
                    select(f, 2)
            pipeline(dve, body)


_INS = ["L0_attn_hidden_states", "L0_attn_w_q", "L0_attn_w_k", "L0_attn_w_v", "L0_attn_w_o", "L0_attn_gate",
        "L0_attn_memory", "L0_attn_memory_norm", "L0_ffn_W_up", "L0_ffn_W_down", "L0_ffn_W_q", "L0_ffn_keys",
        "L0_ffn_down_embed", "L0_ffn_up_embed"]


def kernel(**inputs):
    import numpy as _np
    import concourse.bacc as _bacc
    from concourse.bass_utils import run_bass_kernel_spmd as _run

    nc = _bacc.Bacc("TRN2", target_bir_lowering=False, num_devices=1)
    arrays, args = {}, []
    for name in _INS:
        a = _np.ascontiguousarray(inputs[name])
        arrays[f"in_{name}_dram"] = a
        args.append(nc.dram_tensor(f"in_{name}_dram", a.shape, mybir.dt.from_np(a.dtype), kind="ExternalInput").ap())
    shape = inputs["L0_attn_hidden_states"].shape
    args.append(nc.dram_tensor("out_0_dram", shape, mybir.dt.float32, kind="ExternalOutput").ap())
    sandwich_kernel(nc, *args)
    r = _run(nc, [arrays], core_ids=[0])
    return r.results[0]["out_0_dram"]
```
